# Optimizing a Trainium2 kernel written in Bass

```python
import numpy as np
import jax
import jax.numpy as jnp

def _softmax(x, axis=-1):
    return jax.nn.softmax(x, axis=axis)

def _gelu(x):
    return jax.nn.gelu(x, approximate=True)

def _silu(x):
    return jax.nn.silu(x)

def _sigmoid(x):
    return jax.nn.sigmoid(x)

def _layernorm(x, axis=-1, eps=1e-05):
    m = jnp.mean(x, axis=axis, keepdims=True)
    v = jnp.var(x, axis=axis, keepdims=True)
    return (x - m) / jnp.sqrt(v + eps)

def _scatter_add(tgt, idx, src, axis=0):
    return tgt.at[idx].add(src)

def _segment_sum(src, seg, n):
    return jax.ops.segment_sum(src, seg, n)
kernel_name = 'mk_seq_preln_d1_jaxref_r8_22c363'

def setup_inputs(seed: int=0):
    np.random.seed(seed)
    _w = jnp.asarray

    def _L0_attn_setup():
        import jax, jax.numpy as jnp
        import numpy as np
        DIM = 128
        HEADS = 16
        DIM_HEAD = 64
        SOFTCLAMP = 50.0

        def _rmsnorm(x, w):
            eps = jnp.finfo(x.dtype).eps
            var = jnp.mean(jnp.square(x), axis=-1, keepdims=True)
            return x * jax.lax.rsqrt(var + eps) * w

        def _head_rmsnorm(x, gamma):
            norm = jnp.linalg.norm(x, axis=-1, keepdims=True)
            normed = x / jnp.maximum(norm, 1e-12)
            scale = (gamma + 1.0) * DIM_HEAD ** 0.5
            return normed * scale[None, :, None, :]
        key = jax.random.key(seed)
        ks = jax.random.split(key, 7)
        b, n = (4, 256)
        di = HEADS * DIM_HEAD
        s = 0.02
        return {'tokens': jax.random.normal(ks[0], (b, n, DIM), dtype=jnp.float32), 'norm_w': jnp.ones((DIM,), dtype=jnp.float32), 'Wq': jax.random.normal(ks[1], (DIM, di), dtype=jnp.float32) * s, 'Wkv': jax.random.normal(ks[2], (DIM, 2 * di), dtype=jnp.float32) * s, 'Wo': jax.random.normal(ks[3], (di, DIM), dtype=jnp.float32) * s, 'q_gamma': jnp.zeros((HEADS, DIM_HEAD), dtype=jnp.float32), 'k_gamma': jnp.zeros((HEADS, DIM_HEAD), dtype=jnp.float32)}
    _L0_attn_in = _L0_attn_setup()

    def _L0_ffn_setup():
        import jax, jax.numpy as jnp
        import numpy as np

        def _binarize(w):
            alpha = jax.lax.stop_gradient(jnp.mean(jnp.abs(w), axis=1, keepdims=True))
            bw = alpha * jnp.sign(w)
            return w + jax.lax.stop_gradient(bw - w)
        key = jax.random.key(seed)
        k1, k2, k3, k4, k5 = jax.random.split(key, 5)
        D, H = (128, 512)
        x = jax.random.normal(k1, (64, 196, D), dtype=jnp.float32)
        w1 = jax.random.normal(k2, (H, D), dtype=jnp.float32) * 0.02
        b1 = jax.random.normal(k3, (H,), dtype=jnp.float32) * 0.02
        w2 = jax.random.normal(k4, (D, H), dtype=jnp.float32) * 0.02
        b2 = jax.random.normal(k5, (D,), dtype=jnp.float32) * 0.02
        return {'x': x, 'w1': w1, 'b1': b1, 'w2': w2, 'b2': b2}
    _L0_ffn_in = _L0_ffn_setup()
    _d = {'L0_attn_tokens': _L0_attn_in['tokens'], 'L0_attn_norm_w': _L0_attn_in['norm_w'], 'L0_attn_Wq': _L0_attn_in['Wq'], 'L0_attn_Wkv': _L0_attn_in['Wkv'], 'L0_attn_Wo': _L0_attn_in['Wo'], 'L0_attn_q_gamma': _L0_attn_in['q_gamma'], 'L0_attn_k_gamma': _L0_attn_in['k_gamma'], 'L0_ffn_w1': _L0_ffn_in['w1'], 'L0_ffn_b1': _L0_ffn_in['b1'], 'L0_ffn_w2': _L0_ffn_in['w2'], 'L0_ffn_b2': _L0_ffn_in['b2']}
    _x0 = _d['L0_attn_tokens']
    _d['L0_attn_tokens'] = jax.random.normal(jax.random.fold_in(jax.random.key(seed), 1), (32, 256, 128), dtype=_x0.dtype)
    del _x0
    return _d

def reference(L0_attn_tokens, L0_attn_norm_w, L0_attn_Wq, L0_attn_Wkv, L0_attn_Wo, L0_attn_q_gamma, L0_attn_k_gamma, L0_ffn_w1, L0_ffn_b1, L0_ffn_w2, L0_ffn_b2):

    def _L0_attn_ref(tokens, norm_w, Wq, Wkv, Wo, q_gamma, k_gamma):
        import jax, jax.numpy as jnp
        import numpy as np
        DIM = 128
        HEADS = 16
        DIM_HEAD = 64
        SOFTCLAMP = 50.0

        def _rmsnorm(x, w):
            eps = jnp.finfo(x.dtype).eps
            var = jnp.mean(jnp.square(x), axis=-1, keepdims=True)
            return x * jax.lax.rsqrt(var + eps) * w

        def _head_rmsnorm(x, gamma):
            norm = jnp.linalg.norm(x, axis=-1, keepdims=True)
            normed = x / jnp.maximum(norm, 1e-12)
            scale = (gamma + 1.0) * DIM_HEAD ** 0.5
            return normed * scale[None, :, None, :]
        b, n, _ = tokens.shape
        x = _rmsnorm(tokens, norm_w)
        q = x @ Wq
        kv = x @ Wkv
        k, v = jnp.split(kv, 2, axis=-1)
        split = lambda t: t.reshape(b, n, HEADS, DIM_HEAD).transpose(0, 2, 1, 3)
        q, k, v = (split(q), split(k), split(v))
        q = _head_rmsnorm(q, q_gamma)
        k = _head_rmsnorm(k, k_gamma)
        sim = jnp.einsum('bhid,bhjd->bhij', q, k)
        sim = jnp.tanh(sim / SOFTCLAMP) * SOFTCLAMP
        sim = sim * DIM_HEAD ** (-0.5)
        attn = jax.nn.softmax(sim, axis=-1)
        out = jnp.einsum('bhij,bhjd->bhid', attn, v)
        out = out.transpose(0, 2, 1, 3).reshape(b, n, HEADS * DIM_HEAD)
        return out @ Wo

    def _L0_ffn_ref(x, w1, b1, w2, b2):
        import jax, jax.numpy as jnp
        import numpy as np

        def _binarize(w):
            alpha = jax.lax.stop_gradient(jnp.mean(jnp.abs(w), axis=1, keepdims=True))
            bw = alpha * jnp.sign(w)
            return w + jax.lax.stop_gradient(bw - w)
        bw1 = _binarize(w1)
        h = jnp.einsum('bsd,hd->bsh', x, bw1) + b1
        h = jax.nn.gelu(h, approximate=False)
        bw2 = _binarize(w2)
        out = jnp.einsum('bsh,dh->bsd', h, bw2) + b2
        return out
    x = L0_attn_tokens
    x = x + _L0_attn_ref(_layernorm(x, axis=-1), L0_attn_norm_w, L0_attn_Wq, L0_attn_Wkv, L0_attn_Wo, L0_attn_q_gamma, L0_attn_k_gamma)
    x = x + _L0_ffn_ref(_layernorm(x, axis=-1), L0_ffn_w1, L0_ffn_b1, L0_ffn_w2, L0_ffn_b2)
    return x

_drawn_inputs = setup_inputs


def setup_inputs(seed=0):
    import zlib

    import numpy as np

    out = dict(_drawn_inputs(seed))
    spreads = {'L0_attn_norm_w': (1.0, 0.6), 'L0_attn_q_gamma': (0.0, 0.8), 'L0_attn_k_gamma': (0.0, 0.8)}
    factors = {'L0_attn_Wq': 3.321,
     'L0_attn_Wkv': 2.939,
     'L0_attn_Wo': 2.93,
     'L0_ffn_b1': 8.0,
     'L0_ffn_b2': 2.775}
    for name, (base, spread) in spreads.items():
        noise = np.random.default_rng([zlib.crc32(name.encode()), seed]).standard_normal(out[name].shape)
        drawn = base * np.exp(spread * noise) if base else spread * noise
        out[name] = jnp.asarray(drawn.astype(out[name].dtype))
    for name, factor in factors.items():
        out[name] = (out[name] * factor).astype(out[name].dtype)
    return out
```

```python
import concourse.bass as bass
from concourse import mybir
from contextlib import ExitStack

BATCH, SEQ, DIM = 32, 256, 128
HEADS, DH = 16, 64
HIDDEN = 512
P = 128
TOK = 2 * SEQ
GROUPS = BATCH * SEQ // TOK
NTT = TOK // P
PAIRS = HEADS // 2
INNER = HEADS * DH
QKT = 2 * PAIRS
HT = HIDDEN // P
VECS = 2 * PAIRS + HT + 2
MOM, STEPS = 4, 8
KT = SEQ // P
WSCALE = 64.0
SOFTCLAMP = 50.0
LN_EPS = 1e-5
RMS_EPS = 1.1920928955078125e-07
NORM_FLOOR = 1e-12

PREP, FIN, NORM = "prep", "fin", "norm"


def _norm(j):
    return [(NORM, "nq", j), (NORM, "nk", j)]


def _jobs(group, kind, indices):
    return [(group, kind, i) for i in indices]


SLOTS = [
    (_norm(1), _jobs(PREP, "x", [0]), []),
    (_norm(2) + _jobs(FIN, "ob", range(8)) + _jobs(PREP, "qk", range(0, 4)) + _jobs(FIN, "wo", [0]), [], []),
    (_norm(3) + _jobs(PREP, "ss", [0]) + _jobs(FIN, "ta", [0]) + _jobs(PREP, "v", range(0, 4)), [], []),
    (_norm(4) + _jobs(PREP, "qk", range(4, 8)) + _jobs(FIN, "t2", [0]), [], []),
    (_norm(5) + _jobs(PREP, "ss", [1]) + _jobs(PREP, "v", range(4, 8)) + _jobs(FIN, "h", range(HT)), [], []),
    (_norm(6) + _jobs(PREP, "qk", range(8, 12)), _jobs(FIN, "y", [0]), []),
    (_norm(7) + _jobs(PREP, "ss", [2]) + _jobs(PREP, "qk", range(12, 16)) + _jobs(FIN, "ty", [0]), [],
     _jobs(PREP, "ss", [3])),
    ([], [(PREP, "nq", 0), (PREP, "nk", 0)], []),
]
FIRST = (_jobs(PREP, "x", [0])
         + [job for i in range(4) for job in _jobs(PREP, "qk", range(4 * i, 4 * i + 4))
            + _jobs(PREP, "v", range(2 * i, 2 * i + 2)) + _jobs(PREP, "ss", [i])]
         + [(PREP, "nq", 0), (PREP, "nk", 0)])
LAST = (_jobs(FIN, "ob", range(8)) + _jobs(FIN, "wo", [0]) + _jobs(FIN, "ta", [0]) + _jobs(FIN, "t2", [0])
        + _jobs(FIN, "h", range(HT)) + _jobs(FIN, "y", [0]) + _jobs(FIN, "ty", [0]))


def slot_jobs(slot, prep, fin):
    keep = {NORM: True, PREP: prep, FIN: fin}
    return [[job for job in part if keep[job[0]]] for part in SLOTS[slot]]


def iteration_jobs(prep, fin):
    return [job[1:] for s in range(PAIRS) for part in slot_jobs(s, prep, fin) for job in part]


FULL = iteration_jobs(True, True)
START0 = len(FIRST)
START1 = START0 + len(iteration_jobs(True, False))


def job_number(g, kind, i, prep=True, fin=True):
    at = iteration_jobs(prep, fin).index((kind, i))
    if isinstance(g, int) and g == 0:
        return START0 + at
    return (g - 1) * len(FULL) + (START1 + at)


START_LAST = START1 + (GROUPS - 2) * len(FULL) + len(iteration_jobs(False, True))


def build(nc, x, wq, wkv, wo, w1, w2, vectors, sel32, sel16, out):
    f32, f16, bf16 = mybir.dt.float32, mybir.dt.float16, mybir.dt.bfloat16
    ALU = mybir.AluOpType
    ACT = mybir.ActivationFunctionType
    AX = mybir.AxisListType

    x_g = x.rearrange("(g s) (t p) d -> g p s t d", s=2, p=P)
    out_g = out.rearrange("(g s) (t p) d -> g p s t d", s=2, p=P)

    with ExitStack() as ctx:
        def sb(name, shape, dt=f32):
            return ctx.enter_context(nc.sbuf_tensor(name, shape, dt))

        def sem(name):
            return ctx.enter_context(nc.semaphore(name))

        consts = sb("consts", [P, P + 4 * 32 + PAIRS * 32 + 2])
        ident = consts[:, 0:P]
        sum_sel = consts[:, P:P + 128].rearrange("p (i m) -> p i m", i=4)
        den_sel = consts[:, 2 * P:2 * P + PAIRS * 32].rearrange("p (j m) -> p j m", j=PAIRS)
        neg_mask = consts[:, 2 * P + PAIRS * 32:2 * P + PAIRS * 32 + 2]
        spread = sb("spread", [P, 2, QKT, P], bf16)
        w_hi = sb("w_hi", [P, 3 * INNER], f16)
        w_lo = sb("w_lo", [P, 3 * INNER], f16)
        wo_sb = sb("wo_sb", [P, PAIRS, DIM])
        sgn1T = sb("sgn1T", [P, HIDDEN], f16)
        sgn2T = sb("sgn2T", [P, HT, P])
        small = sb("small", [P, VECS + HT + 1])
        gq, gk = small[:, 0:PAIRS], small[:, PAIRS:2 * PAIRS]
        b1_sb = small[:, 2 * PAIRS:2 * PAIRS + HT]
        b2_sb, nw = small[:, VECS - 2:VECS - 1], small[:, VECS - 1:VECS]
        alpha1, alpha2 = small[:, VECS:VECS + HT], small[:, VECS + HT:VECS + HT + 1]
        minus_half = sb("minus_half", [P, TOK])
        quarter = sb("quarter", [P, 2, NTT])
        x_in = [sb(f"x_in{b}", [P, NTT, DIM]) for b in range(2)]
        stat1 = sb("stat1", [P, NTT, 6])
        mom1 = sb("mom1", [P, MOM, NTT])
        rms1 = sb("rms1", [P, NTT])
        xn = sb("xn", [P, NTT, DIM])
        xT_hi = sb("xT_hi", [P, TOK], f16)
        xT_lo = sb("xT_lo", [P, TOK], f16)
        raw = sb("raw", [P, QKT, TOK])
        squares = sb("squares", [P, 4, TOK])
        sumsq = sb("sumsq", [P, TOK])
        rnorm = sb("rnorm", [P, TOK])
        part_n = sb("part_n", [P, TOK], bf16)
        rn3 = [sb(f"rn3_{b}", [P, TOK], bf16) for b in range(2)]
        v_sb = [sb(f"v_sb{b}", [P, NTT, INNER]) for b in range(2)]
        khat = [sb(f"khat{b}", [P, TOK]) for b in range(2)]
        qhat = [sb(f"qhat{b}", [P, 2, TOK]) for b in range(2)]
        probs = [[sb(f"probs{b}{e}", [P, 2 * KT * SEQ]) for e in range(2)] for b in range(2)]
        o_sb = sb("o_sb", [P, PAIRS, TOK])
        rden = sb("rden", [P, SEQ])
        part_d = sb("part_d", [P, SEQ], bf16)
        rd3 = sb("rd3", [P, SEQ], bf16)
        x_res = sb("x_res", [P, NTT, DIM])
        aT = sb("aT", [P, TOK])
        x1 = sb("x1", [P, NTT, DIM])
        stat2 = sb("stat2", [P, NTT, 6])
        mom2 = sb("mom2", [P, MOM, NTT])
        rstd2 = sb("rstd2", [P, NTT])
        xn2 = sb("xn2", [P, NTT, DIM])
        x2T_hi = sb("x2T_hi", [P, TOK], f16)
        x2T_lo = sb("x2T_lo", [P, TOK], f16)
        hid = sb("hid", [P, HT, TOK])
        yT = sb("yT", [P, TOK])
        out_sb = sb("out_sb", [P, NTT, DIM])

        score = ctx.enter_context(nc.psum_tensor("score", [P, 2, 2 * KT * SEQ], f32))
        work = ctx.enter_context(nc.psum_tensor("work", [P, 2, TOK], f32))
        o_ps = ctx.enter_context(nc.psum_tensor("o_ps", [P, TOK], f32))
        den_ps = ctx.enter_context(nc.psum_tensor("den_ps", [P, 2 * SEQ], f32))

        weights_loaded = sem("weights_loaded")
        setup_step = sem("setup_step")
        signs_turned = sem("signs_turned")
        x_loaded = [sem(f"x_loaded{b}") for b in range(2)]
        res_loaded = sem("res_loaded")
        stored = sem("stored")
        work_full = sem("work_full")
        work_taken = sem("work_taken")
        row_stats1 = sem("row_stats1")
        moments1 = sem("moments1")
        rms1_ready = sem("rms1_ready")
        x_normed = sem("x_normed")
        squared = sem("squared")
        rnorm_ready = sem("rnorm_ready")
        rnorm_parts = sem("rnorm_parts")
        scores_full = sem("scores_full")
        scores_taken = sem("scores_taken")
        probs_ready = sem("probs_ready")
        pv_done = sem("pv_done")
        o_taken = sem("o_taken")
        rden_parts = sem("rden_parts")
        row_stats2 = sem("row_stats2")
        moments2 = sem("moments2")
        rstd2_ready = sem("rstd2_ready")
        x1_normed = sem("x1_normed")
        gelu_done = sem("gelu_done")
        halves_ready = sem("halves_ready")
        x_high = sem("x_high")
        x1_high = sem("x1_high")

        block = ctx.enter_context(nc.Block())
        SETUP_STEPS = 17

        def run(eng, first, iteration, last):
            first()
            iteration(0, 0, True, False)
            with eng.Fori(0, (GROUPS - 2) // 2) as k:
                iteration(k * 2 + 1, 1, True, True)
                iteration(k * 2 + 2, 0, True, True)
            iteration(GROUPS - 1, 1, False, True)
            last()

        @block.sync
        def _(sp):
            flat = raw[:, :, :].rearrange("p t n -> p (t n)")
            sp.dma_start(x_in[0][:, :, :].rearrange("p (s t) d -> p s t d", s=2), x_g[0]).then_inc(x_loaded[0], 16)
            for dst, src in (
                (small[:, 0:VECS], vectors),
                (flat[:, 0:INNER], wq),
                (flat[:, INNER:3 * INNER], wkv),
                (flat[:, 3 * INNER:3 * INNER + HIDDEN].rearrange("p (t d) -> p t d", t=HT),
                 w1.rearrange("(t p) d -> p t d", p=P)),
                (flat[:, 3 * INNER + HIDDEN:3 * INNER + 2 * HIDDEN], w2),
                (consts[:, :], sel32),
                (spread[:, :, :, :].rearrange("p a t m -> p (a t m)"), sel16),
                (wo_sb[:, :, :], wo.rearrange("(j p) d -> p j d", p=P)),
            ):
                sp.dma_start(dst, src).then_inc(weights_loaded, 16)

            def load_x(g, b):
                sp.dma_start(x_in[b][:, :, :].rearrange("p (s t) d -> p s t d", s=2), x_g[g])\
                    .then_inc(x_loaded[b], 16)

            def first():
                load_x(1, 1)

            def store(g):
                sp.dma_start(out_g[g], out_sb[:, :, :].rearrange("p (s t) d -> p s t d", s=2)).then_inc(stored, 16)

            def iteration(g, b, prep, fin):
                if fin:
                    if not (isinstance(g, int) and g == 1):
                        sp.wait_ge(x1_normed, g * NTT - NTT)
                    sp.dma_start(x_res[:, :, :].rearrange("p (s t) d -> p s t d", s=2), x_g[g - 1])\
                        .then_inc(res_loaded, 16)
                if prep and not (isinstance(g, int) and g == GROUPS - 2):
                    sp.wait_ge(x_normed, g * NTT + NTT)
                    load_x(g + 2, b)
                if fin:
                    sp.wait_ge(work_taken, job_number(g, "ty", 0, prep, fin) + 1)
                    store(g - 1)

            first()
            iteration(0, 0, True, False)
            with sp.Fori(0, (GROUPS - 4) // 2) as k:
                iteration(k * 2 + 1, 1, True, True)
                iteration(k * 2 + 2, 0, True, True)
            iteration(GROUPS - 3, 1, True, True)
            iteration(GROUPS - 2, 0, True, True)
            iteration(GROUPS - 1, 1, False, True)
            sp.wait_ge(x1_normed, (GROUPS - 1) * NTT)
            sp.dma_start(x_res[:, :, :].rearrange("p (s t) d -> p s t d", s=2), x_g[GROUPS - 1])\
                .then_inc(res_loaded, 16)
            sp.wait_ge(work_taken, START_LAST + len(LAST))
            store(GROUPS - 1)
            sp.wait_ge(stored, 16 * GROUPS)

        @block.gpsimd
        def _(pool):
            pool.memset(minus_half[:, :], -0.5).then_inc(halves_ready, 1)
            pool.memset(quarter[:, 0, :], 0.25 * (1.0 + RMS_EPS)).then_inc(halves_ready, 1)
            pool.memset(quarter[:, 1, :], 0.25).then_inc(halves_ready, 1)
            pool.wait_ge(halves_ready, 3)

            def row_power(n, stat, mom, scaled, eps, row_stats, steps, ready, result):
                mean, diff, dev, var = (mom[:, i, :] for i in range(MOM))
                fourth = quarter[:, 0 if scaled != 1.0 else 1, :]
                tt, ts = nc.gpsimd.tensor_tensor, nc.gpsimd.tensor_scalar
                pool.wait_ge(row_stats, n * NTT + NTT)
                tt(mean, stat[:, :, 1], stat[:, :, 4], ALU.add).then_inc(steps, 1)
                tt(diff, stat[:, :, 1], stat[:, :, 4], ALU.subtract).then_inc(steps, 1)
                tt(dev, stat[:, :, 2], stat[:, :, 5], ALU.add).then_inc(steps, 1)
                pool.wait_ge(steps, n * STEPS + 3)
                tt(diff, diff, diff, ALU.mult).then_inc(steps, 1)
                ts(mean, mean, 0.5, None, ALU.mult).then_inc(steps, 1)
                ts(dev, dev, scaled / DIM, eps, ALU.mult, ALU.add).then_inc(steps, 1)
                pool.wait_ge(steps, n * STEPS + 6)
                tt(diff, diff, fourth, ALU.mult).then_inc(steps, 1)
                pool.wait_ge(steps, n * STEPS + 7)
                tt(var, dev, diff, ALU.add).then_inc(steps, 1)
                pool.wait_ge(steps, n * STEPS + 8)
                tt(result, var, minus_half[:, 0:NTT], ALU.pow).then_inc(ready, 1)

            def ln1_power(n):
                row_power(n, stat1, mom1, 1.0 + RMS_EPS, RMS_EPS * LN_EPS, row_stats1, moments1, rms1_ready, rms1[:, :])

            def norm_power(n, last_ss):
                pool.wait_ge(work_taken, last_ss + 1)
                if not (isinstance(n, int) and n == 0):
                    pool.wait_ge(rnorm_parts, n * 5)
                nc.gpsimd.tensor_tensor(rnorm[:, :], sumsq[:, :], minus_half[:, :], ALU.pow).then_inc(rnorm_ready, 1)

            def ln2_power(n):
                row_power(n, stat2, mom2, 1.0, LN_EPS, row_stats2, moments2, rstd2_ready, rstd2[:, :])

            def first():
                ln1_power(0)
                norm_power(0, FIRST.index((PREP, "ss", 3)))

            def iteration(g, b, prep, fin):
                if prep:
                    ln1_power(g + 1)
                if fin:
                    ln2_power(g - 1)
                if prep:
                    norm_power(g + 1, job_number(g, "ss", 3, prep, fin))

            def last():
                ln2_power(GROUPS - 1)

            run(pool, first, iteration, last)

        @block.scalar
        def _(act):
            def square(n, tiles, taken, ss_before):
                if ss_before is not None:
                    act.wait_ge(work_full, ss_before + 1)
                for t in tiles:
                    act.wait_ge(work_taken, taken(t) + 1)
                    nc.scalar.activation(squares[:, t % 4, :], raw[:, t, :], ACT.Square).then_inc(squared, 1)

            def gelu(n, last_h):
                act.wait_ge(work_taken, last_h + 1)
                nc.scalar.activation(hid[:, :, :], hid[:, :, :], ACT.Gelu).then_inc(gelu_done, 1)

            def first():
                for i in range(4):
                    square(0, range(4 * i, 4 * i + 4), lambda t: FIRST.index((PREP, "qk", t)),
                           FIRST.index((PREP, "ss", i - 1)) if i else None)

            def iteration(g, b, prep, fin):
                def number(kind, i):
                    return job_number(g, kind, i, prep, fin)

                for j in range(PAIRS):
                    tiles = [i for part in slot_jobs(j, prep, fin) for _, kind, i in part if kind == "qk"]
                    if tiles:
                        i = tiles[0] // 4
                        square(g + 1, tiles, lambda t: number("qk", t), number("ss", i - 1) if i else None)
                    for e in range(2):
                        act.wait_ge(scores_full, g * (2 * PAIRS) + (2 * j + e + 1))
                        if not (isinstance(g, int) and g == 0 and j < 2):
                            act.wait_ge(pv_done, g * PAIRS + (j - 1))
                        nc.scalar.activation(probs[j % 2][e][:, :], score[:, e, :], ACT.Tanh,
                                             scale=1.0 / SOFTCLAMP).then_inc(scores_taken, 1)
                    for e in range(2):
                        act.wait_ge(scores_taken, g * (2 * PAIRS) + (2 * j + e + 1))
                        nc.scalar.activation(probs[j % 2][e][:, :], probs[j % 2][e][:, :], ACT.Exp,
                                             scale=SOFTCLAMP * DH ** -0.5).then_inc(probs_ready, 1)
                    if fin and j == 4:
                        gelu(g - 1, number("h", HT - 1))

            def last():
                gelu(GROUPS - 1, START_LAST + LAST.index((FIN, "h", HT - 1)))

            run(act, first, iteration, last)

        @block.tensor
        def _(pe):
            pe.wait_ge(setup_step, SETUP_STEPS)
            flat = raw[:, :, :].rearrange("p t n -> p (t n)")
            for t in range(HT):
                nc.tensor.transpose(work[:, 0, t * P:(t + 1) * P],
                                    flat[:, 3 * INNER + t * P:3 * INNER + (t + 1) * P], ident)
            for t in range(HT):
                last_turn = nc.tensor.transpose(work[:, 1, t * P:(t + 1) * P],
                                                flat[:, 3 * INNER + HIDDEN + t * P:3 * INNER + HIDDEN + (t + 1) * P],
                                                ident)
            last_turn.then_inc(signs_turned, 1)
            pe.wait_ge(setup_step, SETUP_STEPS + 2)

            def job(n, b, kind, i, group, parity):
                bank = work[:, b, :]
                if not (isinstance(n, int) and n < 2):
                    pe.wait_ge(work_taken, n - 1)
                if kind == "x":
                    pe.wait_ge(x_normed, group * NTT + NTT)
                    for t in range(NTT):
                        mm = nc.tensor.transpose(bank[:, t * P:(t + 1) * P], xn[:, t, :], ident)
                elif kind == "qk":
                    pe.wait_ge(work_taken, x_of(n, i, group) + 1)
                    col = (i % 2) * INNER + (i // 2) * P
                    for s, (w, xt) in enumerate(((w_hi, xT_hi), (w_hi, xT_lo), (w_lo, xT_hi))):
                        mm = nc.tensor.matmul(bank, w[:, col:col + P], xt[:, :], start=(s == 0), stop=(s == 2))
                elif kind == "v":
                    pe.wait_ge(work_taken, x_of(n, i, group) + 1)
                    t, c = i // 2, 2 * INNER + (i % 2) * TOK
                    for s, (xt, w) in enumerate(((xT_hi, w_hi), (xT_lo, w_hi), (xT_hi, w_lo))):
                        mm = nc.tensor.matmul(bank, xt[:, t * P:(t + 1) * P], w[:, c:c + TOK],
                                              start=(s == 0), stop=(s == 2))
                elif kind == "ss":
                    pe.wait_ge(squared, group * QKT + (4 * i + 4))
                    for c in range(4):
                        mm = nc.tensor.matmul(bank[32 * c:32 * c + 32, :], sum_sel[:, i, :], squares[:, c, :],
                                              start=True, stop=True)
                elif kind in ("nq", "nk"):
                    pe.wait_ge(rnorm_parts, group * 5 + 5)
                    mm = nc.tensor.matmul(bank, spread[:, 0, 2 * i + (kind == "nk"), :], rn3[parity][:, :],
                                          start=True, stop=True)
                elif kind == "ob":
                    pe.wait_ge(rden_parts, group * 6 + 6)
                    for s in range(2):
                        mm = nc.tensor.matmul(bank[:, s * SEQ:(s + 1) * SEQ], spread[:, 1, 2 * i + s, :], rd3[:, :],
                                              start=True, stop=True)
                elif kind == "wo":
                    pe.wait_ge(work_taken, ob_of(n) + 1)
                    for j in range(PAIRS):
                        mm = nc.tensor.matmul(bank, wo_sb[:, j, :], o_sb[:, j, :], start=(j == 0),
                                              stop=(j == PAIRS - 1))
                elif kind == "ta":
                    pe.wait_ge(work_taken, of(n, "wo", 0) + 1)
                    for t in range(NTT):
                        mm = nc.tensor.transpose(bank[:, t * P:(t + 1) * P], aT[:, t * P:(t + 1) * P], ident)
                elif kind == "t2":
                    pe.wait_ge(x1_normed, group * NTT + NTT)
                    for t in range(NTT):
                        mm = nc.tensor.transpose(bank[:, t * P:(t + 1) * P], xn2[:, t, :], ident)
                elif kind == "h":
                    pe.wait_ge(work_taken, of(n, "t2", 0) + 1)
                    for s, xt in enumerate((x2T_hi, x2T_lo)):
                        mm = nc.tensor.matmul(bank, sgn1T[:, i * P:(i + 1) * P], xt[:, :], start=(s == 0),
                                              stop=(s == 1))
                elif kind == "y":
                    pe.wait_ge(gelu_done, group + 1)
                    for t in range(HT):
                        mm = nc.tensor.matmul(bank, sgn2T[:, t, :], hid[:, t, :], start=(t == 0), stop=(t == HT - 1))
                elif kind == "ty":
                    pe.wait_ge(work_taken, of(n, "y", 0) + 1)
                    for t in range(NTT):
                        mm = nc.tensor.transpose(bank[:, t * P:(t + 1) * P], yT[:, t * P:(t + 1) * P], ident)
                mm.then_inc(work_full, 1)

            numbers = {}

            def of(n, kind, i):
                return numbers["of"](kind, i)

            def x_of(n, i, group):
                return of(n, "x", 0)

            def ob_of(n):
                return of(n, "ob", PAIRS - 1)

            def scores(g, j, prep, fin):
                if j == 0:
                    n = FIRST.index((PREP, "nk", 0)) if isinstance(g, int) and g == 0 \
                        else job_number_before(g)
                else:
                    n = job_number(g, "nk", j, prep, fin)
                pe.wait_ge(work_taken, n + 1)
                for e in range(2):
                    if not (isinstance(g, int) and g == 0 and j == 0):
                        pe.wait_ge(scores_taken, g * (2 * PAIRS) + (2 * j + e - 1))
                    for s in range(2):
                        for kt in range(KT):
                            c = (s * KT + kt) * SEQ
                            mm = nc.tensor.matmul(score[:, e, c:c + SEQ],
                                                  khat[j % 2][:, s * SEQ + kt * P:s * SEQ + (kt + 1) * P],
                                                  qhat[j % 2][:, e, s * SEQ:(s + 1) * SEQ], start=True, stop=True)
                    mm.then_inc(scores_full, 1)

            def values(g, j, parity):
                pe.wait_ge(probs_ready, g * (2 * PAIRS) + (2 * j + 2))
                if not (isinstance(g, int) and g == 0 and j == 0):
                    pe.wait_ge(o_taken, g * PAIRS + j)
                if j == 0 and not (isinstance(g, int) and g == 0):
                    pe.wait_ge(rden_parts, g * 6 - 5)
                for s in range(2):
                    for kt in range(KT):
                        c = (s * KT + kt) * SEQ
                        for e in range(2):
                            nc.tensor.matmul(o_ps[e * DH:(e + 1) * DH, s * SEQ:(s + 1) * SEQ],
                                             v_sb[parity][:, s * KT + kt, (2 * j + e) * DH:(2 * j + e + 1) * DH],
                                             probs[j % 2][e][:, c:c + SEQ], start=(kt == 0), stop=(kt == KT - 1))
                for kt in range(KT):
                    for s in range(2):
                        c = (s * KT + kt) * SEQ
                        for e in range(2):
                            q = 32 * (2 * e + s)
                            mm = nc.tensor.matmul(den_ps[q:q + 32, 0:SEQ], den_sel[:, j, :],
                                                  probs[j % 2][e][:, c:c + SEQ], start=(j == 0 and kt == 0),
                                                  stop=(j == PAIRS - 1 and kt == KT - 1))
                mm.then_inc(pv_done, 1)

            def job_number_before(g):
                if isinstance(g, int) and g == 1:
                    return job_number(0, "nk", 0, True, False)
                return job_number(g - 1, "nk", 0)

            def first():
                numbers["of"] = lambda kind, i: FIRST.index((PREP, kind, i))
                for n, (_, kind, i) in enumerate(FIRST):
                    job(n, n % 2, kind, i, 0, 0)

            def iteration(g, b, prep, fin):
                numbers["of"] = lambda kind, i: job_number(g, kind, i, prep, fin)
                start = START0 if isinstance(g, int) and g == 0 else START1 + (b == 0) * len(FULL)

                def jobs(part):
                    for kind_of, kind, i in part:
                        at = iteration_jobs(prep, fin).index((kind, i))
                        group = {NORM: g, PREP: g + 1, FIN: g - 1}[kind_of]
                        parity = b if kind_of == NORM else 1 - b
                        job(job_number(g, kind, i, prep, fin), (start + at) % 2, kind, i, group, parity)

                for j in range(PAIRS):
                    before, between, behind = slot_jobs(j, prep, fin)
                    jobs(before)
                    scores(g, j, prep, fin)
                    jobs(between)
                    if j:
                        values(g, j - 1, b)
                    elif not (isinstance(g, int) and g == 0):
                        values(g - 1, PAIRS - 1, 1 - b)
                    jobs(behind)

            def last():
                values(GROUPS - 1, PAIRS - 1, 1)
                numbers["of"] = lambda kind, i: START_LAST + LAST.index((FIN, kind, i))
                for n, (_, kind, i) in enumerate(LAST):
                    job(START_LAST + n, (START_LAST + n) % 2, kind, i, GROUPS - 1, 0)

            run(pe, first, iteration, last)

        @block.vector
        def _(dve):
            flat = raw[:, :, :].rearrange("p t n -> p (t n)")
            w_raw = flat[:, 0:3 * INNER]
            w1_raw = flat[:, 3 * INNER:3 * INNER + HIDDEN]
            w2_raw = flat[:, 3 * INNER + HIDDEN:3 * INNER + 2 * HIDDEN]
            neg1 = squares[:, 0, 0:HIDDEN]
            neg2 = squares[:, 1, 0:HIDDEN]
            dve.wait_ge(weights_loaded, 16 * 8)
            step = [0]

            def done(instruction):
                step[0] += 1
                instruction.then_inc(setup_step, 1)

            done(nc.vector.tensor_scalar(w_raw, w_raw, nw, WSCALE, ALU.mult, ALU.mult))
            done(nc.vector.tensor_scalar(gq, gq, 1.0, DH ** 0.5, ALU.add, ALU.mult))
            done(nc.vector.tensor_scalar(gk, gk, 1.0, DH ** 0.5, ALU.add, ALU.mult))
            done(nc.vector.tensor_reduce(alpha1, w1_raw.rearrange("p (t d) -> p t d", t=HT), AX.X, ALU.add,
                                         apply_absolute_value=True))
            done(nc.vector.tensor_reduce(alpha2, w2_raw, AX.X, ALU.add, apply_absolute_value=True))
            done(nc.vector.tensor_scalar(neg1, w1_raw, 0.0, None, ALU.is_lt))
            done(nc.vector.tensor_scalar(neg2, w2_raw, 0.0, None, ALU.is_lt))
            dve.wait_ge(setup_step, 7)
            done(nc.vector.tensor_copy(w_hi[:, :], w_raw))
            done(nc.vector.tensor_scalar(alpha1, alpha1, 1.0 / DIM, None, ALU.mult))
            done(nc.vector.tensor_scalar(alpha2, alpha2, 1.0 / HIDDEN, None, ALU.mult))
            done(nc.vector.scalar_tensor_tensor(w1_raw, w1_raw, 0.0, neg1, ALU.is_gt, ALU.subtract))
            done(nc.vector.scalar_tensor_tensor(w2_raw, w2_raw, 0.0, neg2, ALU.is_gt, ALU.subtract))
            for b in range(2):
                done(nc.vector.memset(qhat[b][DH:P, 0, :], 0.0))
                done(nc.vector.memset(qhat[b][0:DH, 1, :], 0.0))
            dve.wait_ge(setup_step, 8)
            done(nc.vector.tensor_tensor(w_lo[:, :], w_raw, w_hi[:, :], ALU.subtract))
            assert step[0] == SETUP_STEPS
            dve.wait_ge(signs_turned, 1)
            done(nc.vector.tensor_copy(sgn1T[:, :], work[:, 0, :]))
            done(nc.vector.tensor_copy(sgn2T[:, :, :].rearrange("p t m -> p (t m)"), work[:, 1, :]))
            dve.wait_ge(setup_step, step[0])

            def ln1_stats(n, parity):
                dve.wait_ge(x_loaded[parity], n * 8 + (16 - 8 * parity))
                for t in range(NTT):
                    nc.vector.bn_stats(stat1[:, t, :], x_in[parity][:, t, :]).then_inc(row_stats1, 1)

            def ln1_apply(n, parity):
                dve.wait_ge(rms1_ready, n + 1)
                for t in range(NTT):
                    nc.vector.tensor_scalar(xn[:, t, :], x_in[parity][:, t, :], mom1[:, 0, t:t + 1], rms1[:, t:t + 1],
                                            ALU.subtract, ALU.mult).then_inc(x_normed, 1)

            def split3(target, part, rows, counter, base, at):
                dve.wait_ge(counter, base + at)
                nc.vector.tensor_copy(part, rows).then_inc(counter, 1)
                dve.wait_ge(counter, base + (at + 1))
                nc.vector.scalar_tensor_tensor(rows, part, neg_mask[:, 0:1], rows, ALU.mult, ALU.add)\
                    .then_inc(counter, 1)
                dve.wait_ge(counter, base + (at + 2))
                nc.vector.tensor_copy(part, rows).then_inc(counter, 1)
                dve.wait_ge(counter, base + (at + 3))
                nc.vector.scalar_tensor_tensor(rows, part, neg_mask[:, 1:2], rows, ALU.mult, ALU.add)\
                    .then_inc(counter, 1)
                dve.wait_ge(counter, base + (at + 4))
                nc.vector.tensor_copy(target, rows).then_inc(counter, 1)

            def norm_parts(n, parity):
                dve.wait_ge(rnorm_ready, n + 1)
                split3(rn3[parity][:, :], part_n[:, :], rnorm[:, :], rnorm_parts, n * 5, 0)

            def denominators(n):
                dve.wait_ge(pv_done, n * PAIRS + PAIRS)
                nc.vector.reciprocal(rden[:, :], den_ps[:, 0:SEQ]).then_inc(rden_parts, 1)
                split3(rd3[:, :], part_d[:, :], rden[:, :], rden_parts, n * 6, 1)

            def take(n, b, kind, i, group, parity):
                bank = work[:, b, :]
                dve.wait_ge(work_full, n + 1)
                if kind in ("x", "t2"):
                    hi, lo = (xT_hi, xT_lo) if kind == "x" else (x2T_hi, x2T_lo)
                    high_ready = x_high if kind == "x" else x1_high
                    nc.vector.tensor_copy(hi[:, :], bank).then_inc(high_ready, 1)
                    dve.wait_ge(high_ready, group + 1)
                    last = nc.vector.tensor_tensor(lo[:, :], bank, hi[:, :], ALU.subtract)
                elif kind == "qk":
                    last = nc.vector.tensor_copy(raw[:, i, :], bank)
                elif kind == "v":
                    t, c = i // 2, (i % 2) * TOK
                    last = nc.vector.tensor_scalar(v_sb[parity][:, t, c:c + TOK], bank, 1.0 / WSCALE, None, ALU.mult)
                elif kind == "ss":
                    floor = (NORM_FLOOR * WSCALE) ** 2
                    if i == 0:
                        if not (isinstance(group, int) and group == 0):
                            dve.wait_ge(rnorm_ready, group)
                        last = nc.vector.tensor_scalar(sumsq[:, :], bank, floor, None, ALU.max)
                    else:
                        last = nc.vector.scalar_tensor_tensor(sumsq[:, :], bank, floor, sumsq[:, :], ALU.max, ALU.max)
                elif kind == "nk":
                    last = nc.vector.scalar_tensor_tensor(khat[i % 2][:, :], bank, gk[:, i:i + 1], raw[:, 2 * i + 1, :],
                                                          ALU.mult, ALU.mult)
                elif kind == "nq":
                    for e in range(2):
                        h = slice(e * DH, (e + 1) * DH)
                        last = nc.vector.scalar_tensor_tensor(qhat[i % 2][h, e, :], bank[h, :], gq[h, i:i + 1],
                                                              raw[h, 2 * i, :], ALU.mult, ALU.mult)
                elif kind == "ob":
                    last = nc.vector.tensor_tensor(o_sb[:, i, :], o_sb[:, i, :], bank, ALU.mult)
                elif kind == "wo":
                    last = nc.vector.tensor_copy(aT[:, :], bank)
                elif kind == "ta":
                    dve.wait_ge(res_loaded, group * 16 + 16)
                    last = nc.vector.tensor_tensor(x1[:, :, :].rearrange("p t d -> p (t d)"), bank,
                                                   x_res[:, :, :].rearrange("p t d -> p (t d)"), ALU.add)
                elif kind == "h":
                    last = nc.vector.tensor_scalar(hid[:, i, :], bank, alpha1[:, i:i + 1], b1_sb[:, i:i + 1],
                                                   ALU.mult, ALU.add)
                elif kind == "y":
                    last = nc.vector.tensor_scalar(yT[:, :], bank, alpha2, b2_sb, ALU.mult, ALU.add)
                elif kind == "ty":
                    if not (isinstance(group, int) and group == 0):
                        dve.wait_ge(stored, group * 16)
                    last = nc.vector.tensor_tensor(out_sb[:, :, :].rearrange("p t d -> p (t d)"), bank,
                                                   x1[:, :, :].rearrange("p t d -> p (t d)"), ALU.add)
                last.then_inc(work_taken, 1)
                if kind == "ta":
                    ln2(n, group)
                if kind == "ss" and i == 3:
                    norm_parts(group, parity)

            def ln2(n, group):
                dve.wait_ge(work_taken, n + 1)
                for t in range(NTT):
                    nc.vector.bn_stats(stat2[:, t, :], x1[:, t, :]).then_inc(row_stats2, 1)

            def ln2_apply(group):
                dve.wait_ge(rstd2_ready, group + 1)
                for t in range(NTT):
                    nc.vector.tensor_scalar(xn2[:, t, :], x1[:, t, :], mom2[:, 0, t:t + 1], rstd2[:, t:t + 1],
                                            ALU.subtract, ALU.mult).then_inc(x1_normed, 1)

            def take_o(g, j):
                dve.wait_ge(pv_done, g * PAIRS + (j + 1))
                nc.vector.tensor_copy(o_sb[:, j, :], o_ps[:, :]).then_inc(o_taken, 1)

            def first():
                ln1_stats(0, 0)
                ln1_apply(0, 0)
                for n, (_, kind, i) in enumerate(FIRST):
                    take(n, n % 2, kind, i, 0, 0)

            def iteration(g, b, prep, fin):
                start = START0 if isinstance(g, int) and g == 0 else START1 + (b == 0) * len(FULL)

                def takes(part):
                    for kind_of, kind, i in part:
                        if kind == "t2":
                            ln2_apply(g - 1)
                        at = iteration_jobs(prep, fin).index((kind, i))
                        group = {NORM: g, PREP: g + 1, FIN: g - 1}[kind_of]
                        parity = b if kind_of == NORM else 1 - b
                        take(job_number(g, kind, i, prep, fin), (start + at) % 2, kind, i, group, parity)

                for j in range(PAIRS):
                    before, between, behind = slot_jobs(j, prep, fin)
                    if j == 0 and prep:
                        ln1_stats(g + 1, 1 - b)
                    takes(before)
                    if j == 0 and prep:
                        ln1_apply(g + 1, 1 - b)
                    takes(between)
                    if j:
                        take_o(g, j - 1)
                    elif not (isinstance(g, int) and g == 0):
                        take_o(g - 1, PAIRS - 1)
                        denominators(g - 1)
                    takes(behind)

            def last():
                take_o(GROUPS - 1, PAIRS - 1)
                denominators(GROUPS - 1)
                for n, (_, kind, i) in enumerate(LAST):
                    if kind == "t2":
                        ln2_apply(GROUPS - 1)
                    take(START_LAST + n, (START_LAST + n) % 2, kind, i, GROUPS - 1, 0)

            run(dve, first, iteration, last)


def constants():
    import numpy as np
    s32 = np.zeros((P, P + 128 + PAIRS * 32 + 2), np.float32)
    s32[:, 0:P] = np.eye(P)
    for i in range(4):
        for k in range(4):
            for e in range(2):
                s32[e * DH:(e + 1) * DH, P + i * 32 + 8 * k + 2 * i + e] = 1.0
    for j in range(PAIRS):
        s32[:, 2 * P + 32 * j + j:2 * P + 32 * j + 32:8] = 1.0
    block = (np.arange(P) // 8) % 4
    s32[:, -2] = -1.0 * (block >= 1)
    s32[:, -1] = -1.0 * (block >= 2)
    s16 = np.zeros((P, 2, QKT, P), np.float32)
    for k in range(3):
        for e in range(2):
            cols = slice(e * DH, (e + 1) * DH)
            for t in range(QKT):
                s16[32 * (t % 4) + 8 * k + 2 * (t // 4) + e, 0, t, cols] = 1.0
            for j in range(PAIRS):
                for s in range(2):
                    s16[32 * (2 * e + s) + 8 * k + j, 1, 2 * j + s, cols] = 1.0
    return s32, s16.reshape(P, -1)


def vectors_by_partition(norm_w, q_gamma, k_gamma, b1, b2):
    import numpy as np
    return np.ascontiguousarray(np.concatenate([
        q_gamma.reshape(PAIRS, P).T, k_gamma.reshape(PAIRS, P).T, b1.reshape(HT, P).T,
        b2.reshape(P, 1), norm_w.reshape(P, 1)], axis=1))


def kernel(L0_attn_tokens, L0_attn_norm_w, L0_attn_Wq, L0_attn_Wkv, L0_attn_Wo, L0_attn_q_gamma, L0_attn_k_gamma,
           L0_ffn_w1, L0_ffn_b1, L0_ffn_w2, L0_ffn_b2):
    import numpy as _np
    import ml_dtypes as _ml
    import concourse.bacc as _bacc
    from concourse import mybir as _mybir
    from concourse.bass_utils import run_bass_kernel_spmd as _run

    nc = _bacc.Bacc("TRN2", target_bir_lowering=False, num_devices=1)
    s32, s16 = constants()
    small = [_np.asarray(a) for a in (L0_attn_norm_w, L0_attn_q_gamma, L0_attn_k_gamma, L0_ffn_b1, L0_ffn_b2)]
    given = {
        "tokens": L0_attn_tokens, "Wq": L0_attn_Wq, "Wkv": L0_attn_Wkv, "Wo": L0_attn_Wo,
        "w1": L0_ffn_w1, "w2": L0_ffn_w2, "vectors": vectors_by_partition(*small),
        "sel32": s32, "sel16": s16.astype(_ml.bfloat16),
    }
    arrays, args = {}, []
    for name, a in given.items():
        a = _np.ascontiguousarray(a)
        arrays[f"in_{name}_dram"] = a
        args.append(nc.dram_tensor(f"in_{name}_dram", a.shape, _mybir.dt.from_np(a.dtype), kind="ExternalInput").ap())
    out = nc.dram_tensor("out_dram", (BATCH, SEQ, DIM), _mybir.dt.float32, kind="ExternalOutput").ap()
    build(nc, *args, out)
    r = _run(nc, [arrays], core_ids=[0])
    return r.results[0]["out_dram"]
```

```python
import concourse.bass as bass
from concourse import mybir
from contextlib import ExitStack

BATCH, SEQ, DIM = 32, 256, 128
HEADS, DH = 16, 64
HIDDEN = 512
P = 128
TOK = 2 * SEQ
GROUPS = BATCH * SEQ // TOK
NTT = TOK // P
PAIRS = HEADS // 2
INNER = HEADS * DH
QKT = 2 * PAIRS
HT = HIDDEN // P
VECS = 2 * PAIRS + HT + 2
MOM, STEPS = 4, 8
KT = SEQ // P
WSCALE = 64.0
SOFTCLAMP = 50.0
LN_EPS = 1e-5
RMS_EPS = 1.1920928955078125e-07
NORM_FLOOR = 1e-12
RSQRT_MAGIC = 0x5F3759DF
NEWTON_STEPS = 10

PREP, FIN, NORM = "prep", "fin", "norm"


def _norm(j):
    return [(NORM, "nq", j), (NORM, "nk", j)]


def _jobs(group, kind, indices):
    return [(group, kind, i) for i in indices]


SLOTS = [
    (_norm(1), _jobs(PREP, "x", [0])),
    (_norm(2) + _jobs(FIN, "ob", range(8)) + _jobs(PREP, "qk", range(0, 4)) + _jobs(FIN, "wo", [0]), []),
    (_norm(3) + _jobs(PREP, "ss", [0]) + _jobs(FIN, "ta", [0]) + _jobs(PREP, "v", range(0, 4)), []),
    (_norm(4) + _jobs(PREP, "qk", range(4, 8)) + _jobs(FIN, "t2", [0]), []),
    (_norm(5) + _jobs(PREP, "ss", [1]) + _jobs(PREP, "qk", range(12, 16)) + _jobs(FIN, "h", range(HT)), []),
    (_norm(6) + _jobs(PREP, "ss", [3]) + _jobs(PREP, "qk", range(8, 12)), _jobs(FIN, "y", [0])),
    (_norm(7) + _jobs(PREP, "ss", [2]) + _jobs(PREP, "v", range(4, 8)) + _jobs(FIN, "ty", [0]), []),
    ([(PREP, "nq", 0), (PREP, "nk", 0)], []),
]
SS_ORDER = (0, 1, 3, 2)
BY_SCALAR = ("qk", "v")
FIRST = (_jobs(PREP, "x", [0])
         + [job for n, i in enumerate(SS_ORDER) for job in _jobs(PREP, "qk", range(4 * i, 4 * i + 4))
            + _jobs(PREP, "v", range(2 * n, 2 * n + 2)) + _jobs(PREP, "ss", [i])]
         + [(PREP, "nq", 0), (PREP, "nk", 0)])
LAST = (_jobs(FIN, "ob", range(8)) + _jobs(FIN, "wo", [0]) + _jobs(FIN, "ta", [0]) + _jobs(FIN, "t2", [0])
        + _jobs(FIN, "h", range(HT)) + _jobs(FIN, "y", [0]) + _jobs(FIN, "ty", [0]))


def slot_jobs(slot, prep, fin):
    keep = {NORM: True, PREP: prep, FIN: fin}
    return [[job for job in part if keep[job[0]]] for part in SLOTS[slot]]


def iteration_jobs(prep, fin):
    return [job[1:] for s in range(PAIRS) for part in slot_jobs(s, prep, fin) for job in part]


FULL = iteration_jobs(True, True)
START0 = len(FIRST)
START1 = START0 + len(iteration_jobs(True, False))


assert len(FULL) % 2 == 0


class Job:

    def __init__(self, at, later=0):
        self.number = later * len(FULL) + at
        self.bank = at % 2
        self.turn = later * (len(FULL) // 2) + at // 2


def first_job(kind, i):
    return Job(FIRST.index((PREP, kind, i)))


def job_of(g, kind, i, prep=True, fin=True):
    at = iteration_jobs(prep, fin).index((kind, i))
    if isinstance(g, int) and g == 0:
        return Job(START0 + at)
    return Job(START1 + at, g - 1)


START_LAST = START1 + (GROUPS - 2) * len(FULL) + len(iteration_jobs(False, True))


def last_job(kind, i):
    return Job(START_LAST + LAST.index((FIN, kind, i)))


def raw_place(t, parity):
    return t if t < 12 else t + 4 * parity


def build(nc, x, wq, wkv, wo, w1, w2, vectors, sel32, sel16, out):
    f32, f16, bf16, i32 = mybir.dt.float32, mybir.dt.float16, mybir.dt.bfloat16, mybir.dt.int32
    ALU = mybir.AluOpType
    ACT = mybir.ActivationFunctionType
    AX = mybir.AxisListType

    x_g = x.rearrange("(g s) (t p) d -> g p s t d", s=2, p=P)
    out_g = out.rearrange("(g s) (t p) d -> g p s t d", s=2, p=P)

    with ExitStack() as ctx:
        def sb(name, shape, dt=f32):
            return ctx.enter_context(nc.sbuf_tensor(name, shape, dt))

        def sem(name):
            return ctx.enter_context(nc.semaphore(name))

        consts = sb("consts", [P, P + 4 * 32 + PAIRS * 32 + 2])
        ident = consts[:, 0:P]
        sum_sel = consts[:, P:P + 128].rearrange("p (i m) -> p i m", i=4)
        den_sel = consts[:, 2 * P:2 * P + PAIRS * 32].rearrange("p (j m) -> p j m", j=PAIRS)
        neg_mask = consts[:, 2 * P + PAIRS * 32:2 * P + PAIRS * 32 + 2]
        spread = sb("spread", [P, 2, QKT, P], bf16)
        w_hi = sb("w_hi", [P, 3 * INNER], f16)
        w_lo = sb("w_lo", [P, 3 * INNER], f16)
        wo_sb = sb("wo_sb", [P, PAIRS, DIM])
        sgn1T = sb("sgn1T", [P, HIDDEN], f16)
        sgn2T = sb("sgn2T", [P, HT, P])
        small = sb("small", [P, VECS + HT + 1])
        gq, gk = small[:, 0:PAIRS], small[:, PAIRS:2 * PAIRS]
        b1_sb = small[:, 2 * PAIRS:2 * PAIRS + HT]
        b2_sb, nw = small[:, VECS - 2:VECS - 1], small[:, VECS - 1:VECS]
        alpha1, alpha2 = small[:, VECS:VECS + HT], small[:, VECS + HT:VECS + HT + 1]
        minus_half = sb("minus_half", [P, TOK])
        quarter = sb("quarter", [P, 2, NTT])
        x_in = [sb(f"x_in{b}", [P, NTT, DIM]) for b in range(2)]
        stat1 = sb("stat1", [P, NTT, 6])
        mom1 = sb("mom1", [P, MOM, NTT])
        rms1 = sb("rms1", [P, NTT])
        xn = sb("xn", [P, NTT, DIM])
        xT_hi = sb("xT_hi", [P, TOK], f16)
        xT_lo = sb("xT_lo", [P, TOK], f16)
        raw = sb("raw", [P, QKT + 4, TOK])
        squares = sb("squares", [P, 4, TOK])
        sumsq = sb("sumsq", [P, TOK])
        rnorm = sb("rnorm", [P, TOK])
        newton = sb("newton", [P, TOK])
        part_n = sb("part_n", [P, TOK], bf16)
        rn3 = [sb(f"rn3_{b}", [P, TOK], bf16) for b in range(2)]
        v_sb = [sb(f"v_sb{b}", [P, NTT, INNER]) for b in range(2)]
        k_unit = sb("k_unit", [P, TOK])
        q_unit = sb("q_unit", [P, TOK])
        k_both = [sb(f"k_both{b}", [P, 2, TOK], f16) for b in range(2)]
        q_high = [sb(f"q_high{b}", [P, 2, TOK], f16) for b in range(2)]
        q_low = [sb(f"q_low{b}", [P, 2, TOK], f16) for b in range(2)]
        probs = [[sb(f"probs{b}{e}", [P, 2 * KT * SEQ]) for e in range(2)] for b in range(2)]
        o_sb = sb("o_sb", [P, PAIRS, TOK])
        rden = sb("rden", [P, SEQ])
        part_d = sb("part_d", [P, SEQ], bf16)
        rd3 = sb("rd3", [P, SEQ], bf16)
        x_res = sb("x_res", [P, NTT, DIM])
        aT = sb("aT", [P, TOK])
        x1 = sb("x1", [P, NTT, DIM])
        stat2 = sb("stat2", [P, NTT, 6])
        mom2 = sb("mom2", [P, MOM, NTT])
        rstd2 = sb("rstd2", [P, NTT])
        xn2 = sb("xn2", [P, NTT, DIM])
        x2T_hi = sb("x2T_hi", [P, TOK], f16)
        x2T_lo = sb("x2T_lo", [P, TOK], f16)
        hid = sb("hid", [P, HT, TOK])
        yT = sb("yT", [P, TOK])
        out_sb = sb("out_sb", [P, NTT, DIM])

        score = ctx.enter_context(nc.psum_tensor("score", [P, 2, 2 * KT * SEQ], f32))
        work = ctx.enter_context(nc.psum_tensor("work", [P, 2, TOK], f32))
        o_ps = ctx.enter_context(nc.psum_tensor("o_ps", [P, TOK], f32))
        den_ps = ctx.enter_context(nc.psum_tensor("den_ps", [P, 2 * SEQ], f32))

        weights_loaded = sem("weights_loaded")
        setup_step = sem("setup_step")
        signs_turned = sem("signs_turned")
        x_loaded = [sem(f"x_loaded{b}") for b in range(2)]
        res_loaded = sem("res_loaded")
        stored = sem("stored")
        work_full = sem("work_full")
        work_taken = [sem(f"work_taken{b}") for b in range(2)]
        row_stats1 = sem("row_stats1")
        moments1 = sem("moments1")
        rms1_ready = sem("rms1_ready")
        x_normed = sem("x_normed")
        rnorm_steps = sem("rnorm_steps")
        highs_ready = sem("highs_ready")
        lows_ready = sem("lows_ready")
        rnorm_parts = sem("rnorm_parts")
        scores_full = sem("scores_full")
        scores_taken = sem("scores_taken")
        probs_ready = sem("probs_ready")
        pv_done = sem("pv_done")
        o_taken = sem("o_taken")
        rden_parts = sem("rden_parts")
        row_stats2 = sem("row_stats2")
        moments2 = sem("moments2")
        rstd2_ready = sem("rstd2_ready")
        x1_normed = sem("x1_normed")
        gelu_done = sem("gelu_done")
        halves_ready = sem("halves_ready")
        x_high = sem("x_high")
        x1_high = sem("x1_high")

        block = ctx.enter_context(nc.Block())
        SETUP_STEPS = 17

        def taken(eng, job):
            eng.wait_ge(work_taken[job.bank], job.turn + 1)

        def run(eng, first, iteration, last):
            first()
            iteration(0, 0, True, False)
            with eng.Fori(0, (GROUPS - 2) // 2) as k:
                iteration(k * 2 + 1, 1, True, True)
                iteration(k * 2 + 2, 0, True, True)
            iteration(GROUPS - 1, 1, False, True)
            last()

        @block.sync
        def _(sp):
            flat = raw[:, :, :].rearrange("p t n -> p (t n)")
            sp.dma_start(x_in[0][:, :, :].rearrange("p (s t) d -> p s t d", s=2), x_g[0]).then_inc(x_loaded[0], 16)
            for dst, src in (
                (small[:, 0:VECS], vectors),
                (flat[:, 0:INNER], wq),
                (flat[:, INNER:3 * INNER], wkv),
                (flat[:, 3 * INNER:3 * INNER + HIDDEN].rearrange("p (t d) -> p t d", t=HT),
                 w1.rearrange("(t p) d -> p t d", p=P)),
                (flat[:, 3 * INNER + HIDDEN:3 * INNER + 2 * HIDDEN], w2),
                (consts[:, :], sel32),
                (spread[:, :, :, :].rearrange("p a t m -> p (a t m)"), sel16),
                (wo_sb[:, :, :], wo.rearrange("(j p) d -> p j d", p=P)),
            ):
                sp.dma_start(dst, src).then_inc(weights_loaded, 16)

            def load_x(g, b):
                sp.dma_start(x_in[b][:, :, :].rearrange("p (s t) d -> p s t d", s=2), x_g[g])\
                    .then_inc(x_loaded[b], 16)

            def first():
                load_x(1, 1)

            def store(g):
                sp.dma_start(out_g[g], out_sb[:, :, :].rearrange("p (s t) d -> p s t d", s=2)).then_inc(stored, 16)

            def iteration(g, b, prep, fin):
                if fin:
                    if not (isinstance(g, int) and g == 1):
                        sp.wait_ge(x1_normed, g * NTT - NTT)
                    sp.dma_start(x_res[:, :, :].rearrange("p (s t) d -> p s t d", s=2), x_g[g - 1])\
                        .then_inc(res_loaded, 16)
                if prep and not (isinstance(g, int) and g == GROUPS - 2):
                    sp.wait_ge(x_normed, g * NTT + NTT)
                    load_x(g + 2, b)
                if fin:
                    taken(sp, job_of(g, "ty", 0, prep, fin))
                    store(g - 1)

            first()
            iteration(0, 0, True, False)
            with sp.Fori(0, (GROUPS - 4) // 2) as k:
                iteration(k * 2 + 1, 1, True, True)
                iteration(k * 2 + 2, 0, True, True)
            iteration(GROUPS - 3, 1, True, True)
            iteration(GROUPS - 2, 0, True, True)
            iteration(GROUPS - 1, 1, False, True)
            sp.wait_ge(x1_normed, (GROUPS - 1) * NTT)
            sp.dma_start(x_res[:, :, :].rearrange("p (s t) d -> p s t d", s=2), x_g[GROUPS - 1])\
                .then_inc(res_loaded, 16)
            taken(sp, last_job("ty", 0))
            store(GROUPS - 1)
            sp.wait_ge(stored, 16 * GROUPS)

        @block.gpsimd
        def _(pool):
            pool.memset(minus_half[:, :], -0.5).then_inc(halves_ready, 1)
            pool.memset(quarter[:, 0, :], 0.25 * (1.0 + RMS_EPS)).then_inc(halves_ready, 1)
            pool.memset(quarter[:, 1, :], 0.25).then_inc(halves_ready, 1)
            pool.wait_ge(halves_ready, 3)

            def row_power(n, stat, mom, scaled, eps, row_stats, steps, ready, result):
                mean, diff, dev, var = (mom[:, i, :] for i in range(MOM))
                fourth = quarter[:, 0 if scaled != 1.0 else 1, :]
                tt, ts = nc.gpsimd.tensor_tensor, nc.gpsimd.tensor_scalar
                pool.wait_ge(row_stats, n * NTT + NTT)
                tt(mean, stat[:, :, 1], stat[:, :, 4], ALU.add).then_inc(steps, 1)
                tt(diff, stat[:, :, 1], stat[:, :, 4], ALU.subtract).then_inc(steps, 1)
                tt(dev, stat[:, :, 2], stat[:, :, 5], ALU.add).then_inc(steps, 1)
                pool.wait_ge(steps, n * STEPS + 3)
                tt(diff, diff, diff, ALU.mult).then_inc(steps, 1)
                ts(mean, mean, 0.5, None, ALU.mult).then_inc(steps, 1)
                ts(dev, dev, scaled / DIM, eps, ALU.mult, ALU.add).then_inc(steps, 1)
                pool.wait_ge(steps, n * STEPS + 6)
                tt(diff, diff, fourth, ALU.mult).then_inc(steps, 1)
                pool.wait_ge(steps, n * STEPS + 7)
                tt(var, dev, diff, ALU.add).then_inc(steps, 1)
                pool.wait_ge(steps, n * STEPS + 8)
                tt(result, var, minus_half[:, 0:NTT], ALU.pow).then_inc(ready, 1)
                pool.wait_ge(ready, n + 1)

            def ln1_power(n):
                row_power(n, stat1, mom1, 1.0 + RMS_EPS, RMS_EPS * LN_EPS, row_stats1, moments1, rms1_ready, rms1[:, :])

            def lows(g, j):
                b = j % 2
                pool.wait_ge(highs_ready, (g * PAIRS + j) * 6 + 6)
                for unit, high, low, across in ((k_unit, k_both, k_both, True), (q_unit, q_high, q_low, False)):
                    for e in range(2):
                        own = slice(e * DH, (e + 1) * DH)
                        to = slice((1 - e) * DH, (2 - e) * DH) if across else own
                        nc.gpsimd.tensor_tensor(low[b][to, e, :], unit[own, :], high[b][own, e, :], ALU.subtract)\
                            .then_inc(lows_ready, 1)
                pool.wait_ge(lows_ready, (g * PAIRS + j) * 4 + 4)

            def ln2_power(n):
                row_power(n, stat2, mom2, 1.0, LN_EPS, row_stats2, moments2, rstd2_ready, rstd2[:, :])

            def first():
                ln1_power(0)
                lows(0, 0)

            def iteration(g, b, prep, fin):
                for j in range(PAIRS):
                    if j == 0 and prep:
                        ln1_power(g + 1)
                    if j < PAIRS - 1:
                        lows(g, j + 1)
                    elif prep:
                        lows(g + 1, 0)
                    if j == 2 and fin:
                        ln2_power(g - 1)

            def last():
                ln2_power(GROUPS - 1)

            run(pool, first, iteration, last)

        @block.scalar
        def _(act):
            def take(job, kind, i, parity):
                bank = work[:, job.bank, :]
                act.wait_ge(work_full, job.number + 1)
                if kind == "v":
                    t, c = i // 2, (i % 2) * TOK
                    last_read = nc.scalar.activation(v_sb[parity][:, t, c:c + TOK], bank, ACT.Copy, scale=1.0 / WSCALE)
                else:
                    nc.scalar.activation(raw[:, raw_place(i, parity), :], bank, ACT.Copy)
                    last_read = nc.scalar.activation(squares[:, i % 4, :], bank, ACT.Square)
                last_read.then_inc(work_taken[job.bank], 1)

            def gelu(n, last_h):
                taken(act, last_h)
                nc.scalar.activation(hid[:, :, :], hid[:, :, :], ACT.Gelu).then_inc(gelu_done, 1)

            def take_o(g, j):
                act.wait_ge(pv_done, g * PAIRS + (j + 1))
                nc.scalar.activation(o_sb[:, j, :], o_ps[:, :], ACT.Copy).then_inc(o_taken, 1)

            def first():
                for n, (_, kind, i) in enumerate(FIRST):
                    if kind in BY_SCALAR:
                        take(Job(n), kind, i, 0)

            def iteration(g, b, prep, fin):
                def takes(part):
                    for _, kind, i in part:
                        if kind in BY_SCALAR:
                            take(job_of(g, kind, i, prep, fin), kind, i, 1 - b)

                for j in range(PAIRS):
                    before, between = slot_jobs(j, prep, fin)
                    takes(before)
                    for e in range(2):
                        act.wait_ge(scores_full, g * (2 * PAIRS) + (2 * j + e + 1))
                        if not (isinstance(g, int) and g == 0 and j < 2):
                            act.wait_ge(pv_done, g * PAIRS + (j - 1))
                        nc.scalar.activation(probs[j % 2][e][:, :], score[:, e, :], ACT.Tanh,
                                             scale=1.0 / SOFTCLAMP).then_inc(scores_taken, 1)
                    for e in range(2):
                        act.wait_ge(scores_taken, g * (2 * PAIRS) + (2 * j + e + 1))
                        nc.scalar.activation(probs[j % 2][e][:, :], probs[j % 2][e][:, :], ACT.Exp,
                                             scale=SOFTCLAMP * DH ** -0.5).then_inc(probs_ready, 1)
                    takes(between)
                    if j:
                        take_o(g, j - 1)
                    elif not (isinstance(g, int) and g == 0):
                        take_o(g - 1, PAIRS - 1)
                    if fin and j == 4:
                        gelu(g - 1, job_of(g, "h", HT - 1, prep, fin))

            def last():
                take_o(GROUPS - 1, PAIRS - 1)
                gelu(GROUPS - 1, last_job("h", HT - 1))

            run(act, first, iteration, last)

        @block.tensor
        def _(pe):
            pe.wait_ge(setup_step, SETUP_STEPS)
            flat = raw[:, :, :].rearrange("p t n -> p (t n)")
            for t in range(HT):
                nc.tensor.transpose(work[:, 0, t * P:(t + 1) * P],
                                    flat[:, 3 * INNER + t * P:3 * INNER + (t + 1) * P], ident)
            for t in range(HT):
                last_turn = nc.tensor.transpose(work[:, 1, t * P:(t + 1) * P],
                                                flat[:, 3 * INNER + HIDDEN + t * P:3 * INNER + HIDDEN + (t + 1) * P],
                                                ident)
            last_turn.then_inc(signs_turned, 1)
            pe.wait_ge(setup_step, SETUP_STEPS + 2)

            def job(this, find, kind, i, group, parity):
                bank = work[:, this.bank, :]
                if not (isinstance(this.turn, int) and this.turn == 0):
                    pe.wait_ge(work_taken[this.bank], this.turn)
                if kind == "x":
                    pe.wait_ge(x_normed, group * NTT + NTT)
                    for t in range(NTT):
                        mm = nc.tensor.transpose(bank[:, t * P:(t + 1) * P], xn[:, t, :], ident)
                elif kind == "qk":
                    taken(pe, find("x", 0))
                    col = (i % 2) * INNER + (i // 2) * P
                    for s, (w, xt) in enumerate(((w_hi, xT_hi), (w_hi, xT_lo), (w_lo, xT_hi))):
                        mm = nc.tensor.matmul(bank, w[:, col:col + P], xt[:, :], start=(s == 0), stop=(s == 2))
                elif kind == "v":
                    taken(pe, find("x", 0))
                    t, c = i // 2, 2 * INNER + (i % 2) * TOK
                    for s, (xt, w) in enumerate(((xT_hi, w_hi), (xT_lo, w_hi), (xT_hi, w_lo))):
                        mm = nc.tensor.matmul(bank, xt[:, t * P:(t + 1) * P], w[:, c:c + TOK],
                                              start=(s == 0), stop=(s == 2))
                elif kind == "ss":
                    for t in (4 * i + 2, 4 * i + 3):
                        taken(pe, find("qk", t))
                    for c in range(4):
                        mm = nc.tensor.matmul(bank[32 * c:32 * c + 32, :], sum_sel[:, i, :], squares[:, c, :],
                                              start=True, stop=True)
                elif kind in ("nq", "nk"):
                    pe.wait_ge(rnorm_parts, group * 5 + 5)
                    mm = nc.tensor.matmul(bank, spread[:, 0, 2 * i + (kind == "nk"), :], rn3[parity][:, :],
                                          start=True, stop=True)
                elif kind == "ob":
                    pe.wait_ge(rden_parts, group * 6 + 6)
                    for s in range(2):
                        mm = nc.tensor.matmul(bank[:, s * SEQ:(s + 1) * SEQ], spread[:, 1, 2 * i + s, :], rd3[:, :],
                                              start=True, stop=True)
                elif kind == "wo":
                    for j in (PAIRS - 2, PAIRS - 1):
                        taken(pe, find("ob", j))
                    for j in range(PAIRS):
                        mm = nc.tensor.matmul(bank, wo_sb[:, j, :], o_sb[:, j, :], start=(j == 0),
                                              stop=(j == PAIRS - 1))
                elif kind == "ta":
                    taken(pe, find("wo", 0))
                    for t in range(NTT):
                        mm = nc.tensor.transpose(bank[:, t * P:(t + 1) * P], aT[:, t * P:(t + 1) * P], ident)
                elif kind == "t2":
                    pe.wait_ge(x1_normed, group * NTT + NTT)
                    for t in range(NTT):
                        mm = nc.tensor.transpose(bank[:, t * P:(t + 1) * P], xn2[:, t, :], ident)
                elif kind == "h":
                    taken(pe, find("t2", 0))
                    for s, xt in enumerate((x2T_hi, x2T_lo)):
                        mm = nc.tensor.matmul(bank, sgn1T[:, i * P:(i + 1) * P], xt[:, :], start=(s == 0),
                                              stop=(s == 1))
                elif kind == "y":
                    pe.wait_ge(gelu_done, group + 1)
                    for t in range(HT):
                        mm = nc.tensor.matmul(bank, sgn2T[:, t, :], hid[:, t, :], start=(t == 0), stop=(t == HT - 1))
                elif kind == "ty":
                    taken(pe, find("y", 0))
                    for t in range(NTT):
                        mm = nc.tensor.transpose(bank[:, t * P:(t + 1) * P], yT[:, t * P:(t + 1) * P], ident)
                mm.then_inc(work_full, 1)

            def scores(g, j):
                pe.wait_ge(lows_ready, (g * PAIRS + j) * 4 + 4)
                for e in range(2):
                    if not (isinstance(g, int) and g == 0 and j == 0):
                        pe.wait_ge(scores_taken, g * (2 * PAIRS) + (2 * j + e - 1))
                    for s in range(2):
                        for kt in range(KT):
                            c = (s * KT + kt) * SEQ
                            keys = k_both[j % 2][:, e, s * SEQ + kt * P:s * SEQ + (kt + 1) * P]
                            nc.tensor.matmul(score[:, e, c:c + SEQ], keys, q_high[j % 2][:, e, s * SEQ:(s + 1) * SEQ],
                                             start=True, stop=False)
                            mm = nc.tensor.matmul(score[:, e, c:c + SEQ], keys,
                                                  q_low[j % 2][:, e, s * SEQ:(s + 1) * SEQ], start=False, stop=True)
                    mm.then_inc(scores_full, 1)

            def values(g, j, parity):
                pe.wait_ge(probs_ready, g * (2 * PAIRS) + (2 * j + 2))
                if not (isinstance(g, int) and g == 0 and j == 0):
                    pe.wait_ge(o_taken, g * PAIRS + j)
                if j == 0 and not (isinstance(g, int) and g == 0):
                    pe.wait_ge(rden_parts, g * 6 - 5)
                for s in range(2):
                    for kt in range(KT):
                        c = (s * KT + kt) * SEQ
                        for e in range(2):
                            nc.tensor.matmul(o_ps[e * DH:(e + 1) * DH, s * SEQ:(s + 1) * SEQ],
                                             v_sb[parity][:, s * KT + kt, (2 * j + e) * DH:(2 * j + e + 1) * DH],
                                             probs[j % 2][e][:, c:c + SEQ], start=(kt == 0), stop=(kt == KT - 1))
                for kt in range(KT):
                    for s in range(2):
                        c = (s * KT + kt) * SEQ
                        for e in range(2):
                            q = 32 * (2 * e + s)
                            mm = nc.tensor.matmul(den_ps[q:q + 32, 0:SEQ], den_sel[:, j, :],
                                                  probs[j % 2][e][:, c:c + SEQ], start=(j == 0 and kt == 0),
                                                  stop=(j == PAIRS - 1 and kt == KT - 1))
                mm.then_inc(pv_done, 1)

            def first():
                for n, (_, kind, i) in enumerate(FIRST):
                    job(Job(n), first_job, kind, i, 0, 0)

            def iteration(g, b, prep, fin):
                def find(kind, i):
                    return job_of(g, kind, i, prep, fin)

                def jobs(part):
                    for kind_of, kind, i in part:
                        group = {NORM: g, PREP: g + 1, FIN: g - 1}[kind_of]
                        job(find(kind, i), find, kind, i, group, b if kind_of == NORM else 1 - b)

                for j in range(PAIRS):
                    before, between = slot_jobs(j, prep, fin)
                    jobs(before)
                    scores(g, j)
                    jobs(between)
                    if j:
                        values(g, j - 1, b)
                    elif not (isinstance(g, int) and g == 0):
                        values(g - 1, PAIRS - 1, 1 - b)

            def last():
                values(GROUPS - 1, PAIRS - 1, 1)
                for _, kind, i in LAST:
                    job(last_job(kind, i), last_job, kind, i, GROUPS - 1, 0)

            run(pe, first, iteration, last)

        @block.vector
        def _(dve):
            flat = raw[:, :, :].rearrange("p t n -> p (t n)")
            w_raw = flat[:, 0:3 * INNER]
            w1_raw = flat[:, 3 * INNER:3 * INNER + HIDDEN]
            w2_raw = flat[:, 3 * INNER + HIDDEN:3 * INNER + 2 * HIDDEN]
            neg1 = squares[:, 0, 0:HIDDEN]
            neg2 = squares[:, 1, 0:HIDDEN]
            dve.wait_ge(weights_loaded, 16 * 8)
            step = [0]

            def done(instruction):
                step[0] += 1
                instruction.then_inc(setup_step, 1)

            done(nc.vector.tensor_scalar(w_raw, w_raw, nw, WSCALE, ALU.mult, ALU.mult))
            done(nc.vector.tensor_scalar(gq, gq, 1.0, DH ** 0.5, ALU.add, ALU.mult))
            done(nc.vector.tensor_scalar(gk, gk, 1.0, DH ** 0.5, ALU.add, ALU.mult))
            done(nc.vector.tensor_reduce(alpha1, w1_raw.rearrange("p (t d) -> p t d", t=HT), AX.X, ALU.add,
                                         apply_absolute_value=True))
            done(nc.vector.tensor_reduce(alpha2, w2_raw, AX.X, ALU.add, apply_absolute_value=True))
            done(nc.vector.tensor_scalar(neg1, w1_raw, 0.0, None, ALU.is_lt))
            done(nc.vector.tensor_scalar(neg2, w2_raw, 0.0, None, ALU.is_lt))
            dve.wait_ge(setup_step, 7)
            done(nc.vector.tensor_copy(w_hi[:, :], w_raw))
            done(nc.vector.tensor_scalar(alpha1, alpha1, 1.0 / DIM, None, ALU.mult))
            done(nc.vector.tensor_scalar(alpha2, alpha2, 1.0 / HIDDEN, None, ALU.mult))
            done(nc.vector.scalar_tensor_tensor(w1_raw, w1_raw, 0.0, neg1, ALU.is_gt, ALU.subtract))
            done(nc.vector.scalar_tensor_tensor(w2_raw, w2_raw, 0.0, neg2, ALU.is_gt, ALU.subtract))
            for b in range(2):
                done(nc.vector.memset(q_low[b][DH:P, 0, :], 0.0))
                done(nc.vector.memset(q_low[b][0:DH, 1, :], 0.0))
            dve.wait_ge(setup_step, 8)
            done(nc.vector.tensor_tensor(w_lo[:, :], w_raw, w_hi[:, :], ALU.subtract))
            assert step[0] == SETUP_STEPS
            dve.wait_ge(signs_turned, 1)
            done(nc.vector.tensor_copy(sgn1T[:, :], work[:, 0, :]))
            done(nc.vector.tensor_copy(sgn2T[:, :, :].rearrange("p t m -> p (t m)"), work[:, 1, :]))
            dve.wait_ge(setup_step, step[0])

            def ln1_stats(n, parity):
                dve.wait_ge(x_loaded[parity], n * 8 + (16 - 8 * parity))
                for t in range(NTT):
                    nc.vector.bn_stats(stat1[:, t, :], x_in[parity][:, t, :]).then_inc(row_stats1, 1)

            def ln1_apply(n, parity):
                dve.wait_ge(rms1_ready, n + 1)
                for t in range(NTT):
                    nc.vector.tensor_scalar(xn[:, t, :], x_in[parity][:, t, :], mom1[:, 0, t:t + 1], rms1[:, t:t + 1],
                                            ALU.subtract, ALU.mult).then_inc(x_normed, 1)

            def split3(target, part, rows, counter, base, at):
                if at:
                    dve.wait_ge(counter, base + at)
                nc.vector.tensor_copy(part, rows).then_inc(counter, 1)
                dve.wait_ge(counter, base + (at + 1))
                nc.vector.scalar_tensor_tensor(rows, part, neg_mask[:, 0:1], rows, ALU.mult, ALU.add)\
                    .then_inc(counter, 1)
                dve.wait_ge(counter, base + (at + 2))
                nc.vector.tensor_copy(part, rows).then_inc(counter, 1)
                dve.wait_ge(counter, base + (at + 3))
                nc.vector.scalar_tensor_tensor(rows, part, neg_mask[:, 1:2], rows, ALU.mult, ALU.add)\
                    .then_inc(counter, 1)
                dve.wait_ge(counter, base + (at + 4))
                nc.vector.tensor_copy(target, rows).then_inc(counter, 1)

            def norm_parts(n, parity, last_ss):
                base = n * NEWTON_STEPS
                taken(dve, last_ss)
                nc.vector.tensor_scalar(rnorm[:, :].bitcast(i32), sumsq[:, :].bitcast(i32), -0.5, float(RSQRT_MAGIC),
                                        ALU.mult, ALU.add).then_inc(rnorm_steps, 1)
                for step_n in range(3):
                    at = base + 3 * step_n
                    dve.wait_ge(rnorm_steps, at + 1)
                    nc.vector.scalar_tensor_tensor(newton[:, :], rnorm[:, :], -0.5, rnorm[:, :], ALU.mult, ALU.mult)\
                        .then_inc(rnorm_steps, 1)
                    dve.wait_ge(rnorm_steps, at + 2)
                    nc.vector.tensor_tensor(newton[:, :], newton[:, :], sumsq[:, :], ALU.mult)\
                        .then_inc(rnorm_steps, 1)
                    dve.wait_ge(rnorm_steps, at + 3)
                    nc.vector.scalar_tensor_tensor(rnorm[:, :], newton[:, :], 1.5, rnorm[:, :], ALU.add, ALU.mult)\
                        .then_inc(rnorm_steps, 1)
                dve.wait_ge(rnorm_steps, base + NEWTON_STEPS)
                split3(rn3[parity][:, :], part_n[:, :], rnorm[:, :], rnorm_parts, n * 5, 0)

            def halves(g, j):
                b = j % 2
                u = g * PAIRS + j
                for unit, high in ((k_unit, k_both), (q_unit, q_high)):
                    for e in range(2):
                        own = slice(e * DH, (e + 1) * DH)
                        nc.vector.tensor_copy(high[b][own, e, :], unit[own, :]).then_inc(highs_ready, 1)
                dve.wait_ge(highs_ready, u * 6 + 4)
                for e in range(2):
                    own, far = slice(e * DH, (e + 1) * DH), slice((1 - e) * DH, (2 - e) * DH)
                    nc.vector.tensor_copy(q_high[b][far, e, :], q_high[b][own, e, :]).then_inc(highs_ready, 1)

            def denominators(n):
                dve.wait_ge(pv_done, n * PAIRS + PAIRS)
                nc.vector.reciprocal(rden[:, :], den_ps[:, 0:SEQ]).then_inc(rden_parts, 1)
                split3(rd3[:, :], part_d[:, :], rden[:, :], rden_parts, n * 6, 1)

            def take(job, kind, i, group, parity):
                bank = work[:, job.bank, :]
                dve.wait_ge(work_full, job.number + 1)
                if kind in ("x", "t2"):
                    hi, lo = (xT_hi, xT_lo) if kind == "x" else (x2T_hi, x2T_lo)
                    high_ready = x_high if kind == "x" else x1_high
                    nc.vector.tensor_copy(hi[:, :], bank).then_inc(high_ready, 1)
                    dve.wait_ge(high_ready, group + 1)
                    last = nc.vector.tensor_tensor(lo[:, :], bank, hi[:, :], ALU.subtract)
                elif kind == "ss":
                    floor = (NORM_FLOOR * WSCALE) ** 2
                    if i == 0:
                        last = nc.vector.tensor_scalar(sumsq[:, :], bank, floor, None, ALU.max)
                    else:
                        last = nc.vector.scalar_tensor_tensor(sumsq[:, :], bank, floor, sumsq[:, :], ALU.max, ALU.max)
                elif kind in ("nq", "nk"):
                    unit, gamma, t = (q_unit, gq, 2 * i) if kind == "nq" else (k_unit, gk, 2 * i + 1)
                    if kind == "nq" and not (isinstance(group, int) and group == 0 and i == 0):
                        dve.wait_ge(lows_ready, (group * PAIRS + i) * 4)
                    last = nc.vector.scalar_tensor_tensor(unit[:, :], bank, gamma[:, i:i + 1],
                                                          raw[:, raw_place(t, parity), :], ALU.mult, ALU.mult)
                elif kind == "ob":
                    if i == 0:
                        dve.wait_ge(o_taken, group * PAIRS + PAIRS)
                    last = nc.vector.tensor_tensor(o_sb[:, i, :], o_sb[:, i, :], bank, ALU.mult)
                elif kind == "wo":
                    last = nc.vector.tensor_copy(aT[:, :], bank)
                elif kind == "ta":
                    dve.wait_ge(res_loaded, group * 16 + 16)
                    last = nc.vector.tensor_tensor(x1[:, :, :].rearrange("p t d -> p (t d)"), bank,
                                                   x_res[:, :, :].rearrange("p t d -> p (t d)"), ALU.add)
                elif kind == "h":
                    last = nc.vector.tensor_scalar(hid[:, i, :], bank, alpha1[:, i:i + 1], b1_sb[:, i:i + 1],
                                                   ALU.mult, ALU.add)
                elif kind == "y":
                    last = nc.vector.tensor_scalar(yT[:, :], bank, alpha2, b2_sb, ALU.mult, ALU.add)
                elif kind == "ty":
                    if not (isinstance(group, int) and group == 0):
                        dve.wait_ge(stored, group * 16)
                    last = nc.vector.tensor_tensor(out_sb[:, :, :].rearrange("p t d -> p (t d)"), bank,
                                                   x1[:, :, :].rearrange("p t d -> p (t d)"), ALU.add)
                last.then_inc(work_taken[job.bank], 1)
                if kind == "ta":
                    ln2(job, group)
                if kind == "ss" and i == SS_ORDER[-1]:
                    norm_parts(group, parity, job)

            def ln2(job, group):
                taken(dve, job)
                for t in range(NTT):
                    nc.vector.bn_stats(stat2[:, t, :], x1[:, t, :]).then_inc(row_stats2, 1)

            def ln2_apply(group):
                dve.wait_ge(rstd2_ready, group + 1)
                for t in range(NTT):
                    nc.vector.tensor_scalar(xn2[:, t, :], x1[:, t, :], mom2[:, 0, t:t + 1], rstd2[:, t:t + 1],
                                            ALU.subtract, ALU.mult).then_inc(x1_normed, 1)

            def first():
                ln1_stats(0, 0)
                ln1_apply(0, 0)
                for n, (_, kind, i) in enumerate(FIRST):
                    if kind not in BY_SCALAR:
                        take(Job(n), kind, i, 0, 0)
                units_landed(first_job("nq", 0), first_job("nk", 0))
                halves(0, 0)

            def units_landed(*jobs):
                for job in jobs:
                    taken(dve, job)

            def iteration(g, b, prep, fin):
                def takes(part):
                    for kind_of, kind, i in part:
                        if kind in BY_SCALAR:
                            continue
                        if kind == "t2":
                            ln2_apply(g - 1)
                        group = {NORM: g, PREP: g + 1, FIN: g - 1}[kind_of]
                        take(job_of(g, kind, i, prep, fin), kind, i, group, b if kind_of == NORM else 1 - b)
                        if kind == "nk":
                            units_landed(job_of(g, "nq", i, prep, fin), job_of(g, "nk", i, prep, fin))
                            halves(group, i)

                for j in range(PAIRS):
                    before, between = slot_jobs(j, prep, fin)
                    if j == 0 and prep:
                        ln1_stats(g + 1, 1 - b)
                    takes(before)
                    if j == 0 and prep:
                        ln1_apply(g + 1, 1 - b)
                    takes(between)
                    if j == 0 and not (isinstance(g, int) and g == 0):
                        denominators(g - 1)

            def last():
                denominators(GROUPS - 1)
                for _, kind, i in LAST:
                    if kind == "t2":
                        ln2_apply(GROUPS - 1)
                    take(last_job(kind, i), kind, i, GROUPS - 1, 0)

            run(dve, first, iteration, last)


def constants():
    import numpy as np
    s32 = np.zeros((P, P + 128 + PAIRS * 32 + 2), np.float32)
    s32[:, 0:P] = np.eye(P)
    for i in range(4):
        for k in range(4):
            for e in range(2):
                s32[e * DH:(e + 1) * DH, P + i * 32 + 8 * k + 2 * i + e] = 1.0
    for j in range(PAIRS):
        s32[:, 2 * P + 32 * j + j:2 * P + 32 * j + 32:8] = 1.0
    block = (np.arange(P) // 8) % 4
    s32[:, -2] = -1.0 * (block >= 1)
    s32[:, -1] = -1.0 * (block >= 2)
    s16 = np.zeros((P, 2, QKT, P), np.float32)
    for k in range(3):
        for e in range(2):
            cols = slice(e * DH, (e + 1) * DH)
            for t in range(QKT):
                s16[32 * (t % 4) + 8 * k + 2 * (t // 4) + e, 0, t, cols] = 1.0
            for j in range(PAIRS):
                for s in range(2):
                    s16[32 * (2 * e + s) + 8 * k + j, 1, 2 * j + s, cols] = 1.0
    return s32, s16.reshape(P, -1)


def vectors_by_partition(norm_w, q_gamma, k_gamma, b1, b2):
    import numpy as np
    return np.ascontiguousarray(np.concatenate([
        q_gamma.reshape(PAIRS, P).T, k_gamma.reshape(PAIRS, P).T, b1.reshape(HT, P).T,
        b2.reshape(P, 1), norm_w.reshape(P, 1)], axis=1))


def kernel(L0_attn_tokens, L0_attn_norm_w, L0_attn_Wq, L0_attn_Wkv, L0_attn_Wo, L0_attn_q_gamma, L0_attn_k_gamma,
           L0_ffn_w1, L0_ffn_b1, L0_ffn_w2, L0_ffn_b2):
    import numpy as _np
    import ml_dtypes as _ml
    import concourse.bacc as _bacc
    from concourse import mybir as _mybir
    from concourse.bass_utils import run_bass_kernel_spmd as _run

    nc = _bacc.Bacc("TRN2", target_bir_lowering=False, num_devices=1)
    s32, s16 = constants()
    small = [_np.asarray(a) for a in (L0_attn_norm_w, L0_attn_q_gamma, L0_attn_k_gamma, L0_ffn_b1, L0_ffn_b2)]
    given = {
        "tokens": L0_attn_tokens, "Wq": L0_attn_Wq, "Wkv": L0_attn_Wkv, "Wo": L0_attn_Wo,
        "w1": L0_ffn_w1, "w2": L0_ffn_w2, "vectors": vectors_by_partition(*small),
        "sel32": s32, "sel16": s16.astype(_ml.bfloat16),
    }
    arrays, args = {}, []
    for name, a in given.items():
        a = _np.ascontiguousarray(a)
        arrays[f"in_{name}_dram"] = a
        args.append(nc.dram_tensor(f"in_{name}_dram", a.shape, _mybir.dt.from_np(a.dtype), kind="ExternalInput").ap())
    out = nc.dram_tensor("out_dram", (BATCH, SEQ, DIM), _mybir.dt.float32, kind="ExternalOutput").ap()
    build(nc, *args, out)
    r = _run(nc, [arrays], core_ids=[0])
    return r.results[0]["out_dram"]
```

```python
import concourse.bass as bass
from concourse import mybir
from contextlib import ExitStack

BATCH, SEQ, DIM = 32, 256, 128
HEADS, DH = 16, 64
HIDDEN = 512
P = 128
TOK = 2 * SEQ
GROUPS = BATCH * SEQ // TOK
NTT = TOK // P
PAIRS = HEADS // 2
INNER = HEADS * DH
QKT = 2 * PAIRS
HT = HIDDEN // P
VECS = 2 * PAIRS + HT + 2
MOM, STEPS = 4, 8
KT = SEQ // P
WSCALE = 64.0
SOFTCLAMP = 50.0
LN_EPS = 1e-5
RMS_EPS = 1.1920928955078125e-07
NORM_FLOOR = 1e-12
RSQRT_MAGIC = 0x5F3759DF
NEWTON_STEPS = 10

PHASES = 7
PREP, FIN, NORM = "prep", "fin", "norm"


def _jobs(group, kind, *indices):
    return [(group, kind, i) for i in indices]


def _norm(group, j):
    return [(group, "nq", j), (group, "nk", j)]


SLOTS = [
    [[], [], [], [], [], _jobs(PREP, "x", 0), _jobs(NORM, "nq", 2) + _jobs(NORM, "nk", 2)],
    [_jobs(PREP, "qk", 0), [], _jobs(PREP, "qk", 1) + _jobs(PREP, "v", 0), _jobs(PREP, "qk", 2), _jobs(FIN, "ob", 3),
     _jobs(FIN, "ob", 7, 0, 2) + _jobs(NORM, "nq", 3) + _jobs(NORM, "nk", 3), _jobs(PREP, "qk", 3)],
    [[], [], _jobs(FIN, "ob", 4) + _jobs(PREP, "ss", 0) + _jobs(PREP, "qk", 4), _jobs(PREP, "qk", 5),
     _jobs(FIN, "ob", 5), _jobs(FIN, "ob", 1) + _jobs(PREP, "qk", 7), _jobs(NORM, "nq", 4)],
    [[], _jobs(FIN, "ob", 6) + _jobs(NORM, "nk", 4), _jobs(PREP, "qk", 6), [],
     _jobs(PREP, "v", 1) + _jobs(FIN, "wo", 0), _jobs(PREP, "ss", 1) + _jobs(NORM, "nq", 5),
     _jobs(PREP, "qk", 15, 13)],
    [_jobs(FIN, "ta", 0) + _jobs(PREP, "qk", 14) + _jobs(NORM, "nk", 5), [], [], _jobs(PREP, "qk", 12), [],
     _jobs(PREP, "ss", 3) + _jobs(PREP, "qk", 11), _jobs(NORM, "nq", 6) + _jobs(NORM, "nk", 6)],
    [_jobs(PREP, "qk", 9, 10), [], _jobs(PREP, "qk", 8), [], _jobs(FIN, "t2", 0),
     _jobs(PREP, "v", 2) + _jobs(PREP, "ss", 2) + _jobs(FIN, "h", 0) + _jobs(PREP, "v", 3),
     _jobs(FIN, "h", 1) + _jobs(NORM, "nq", 7) + _jobs(NORM, "nk", 7)],
    [_jobs(PREP, "v", 4) + _jobs(FIN, "h", 2), [], [], [], _jobs(PREP, "v", 5) + _jobs(FIN, "h", 3), [],
     _jobs(PREP, "v", 6)],
    [_jobs(PREP, "v", 7), [], _jobs(PREP, "nq", 0) + _jobs(PREP, "nk", 0), [], _jobs(FIN, "y", 0),
     _jobs(PREP, "nq", 1) + _jobs(FIN, "ty", 0), _jobs(PREP, "nk", 1)],
]
VECTOR_WORK = {
    (0, 6): ["den_reciprocal"],
    (1, 0): ["den_parts0", "den_parts1"],
    (5, 5): ["newton0", "newton1"],
    (5, 6): ["newton2"],
    (6, 0): ["newton3"],
    (6, 1): ["newton4", "newton5"],
    (6, 2): ["newton6"],
    (6, 3): ["newton7", "newton8"],
    (6, 4): ["parts0", "parts1"],
    (6, 6): ["stats"],
    (7, 5): ["apply"],
}
LN1_POWER_AT, LN2_POWER_AT = (6, "sums"), (3, "sums")
GELU_AT = (6, 6)
PART_STEPS = (range(0, 2), range(2, 5))
SS_ORDER = (0, 1, 3, 2)
BY_SCALAR = ("qk", "v")
FIRST = (_jobs(PREP, "x", 0)
         + _jobs(PREP, "qk", 0, 1, 2, 3) + _jobs(PREP, "v", 0) + _jobs(PREP, "ss", 0)
         + _jobs(PREP, "qk", 4, 5, 6, 7) + _jobs(PREP, "v", 1) + _jobs(PREP, "ss", 1)
         + _jobs(PREP, "qk", 12, 13, 14, 15) + _jobs(PREP, "v", 2) + _jobs(PREP, "ss", 3)
         + _jobs(PREP, "qk", 8, 9, 10, 11) + _norm(PREP, 0) + _jobs(PREP, "ss", 2)
         + _norm(PREP, 1) + _jobs(PREP, "v", 3, 4, 5, 6, 7))
LAST = (_jobs(FIN, "ob", *range(8)) + _jobs(FIN, "wo", 0) + _jobs(FIN, "ta", 0) + _jobs(FIN, "t2", 0)
        + _jobs(FIN, "h", *range(HT)) + _jobs(FIN, "y", 0) + _jobs(FIN, "ty", 0))


def slot_jobs(slot, prep, fin):
    keep = {NORM: True, PREP: prep, FIN: fin}
    return [[job for job in part if keep[job[0]]] for part in SLOTS[slot]]


def iteration_jobs(prep, fin):
    return [job[1:] for s in range(PAIRS) for part in slot_jobs(s, prep, fin) for job in part]


FULL = iteration_jobs(True, True)
START0 = len(FIRST)
START1 = START0 + len(iteration_jobs(True, False))
assert len(FULL) % 2 == 0


EARLY_PAIRS = 4


def early(group, j):
    return isinstance(group, int) and group == 0 and j < EARLY_PAIRS


class Job:

    def __init__(self, at, later=0):
        self.at = at
        self.number = later * len(FULL) + at
        self.bank = at % 2
        self.turn = later * (len(FULL) // 2) + at // 2


def first_job(kind, i):
    return Job(FIRST.index((PREP, kind, i)))


def job_of(g, kind, i, prep=True, fin=True):
    at = iteration_jobs(prep, fin).index((kind, i))
    if isinstance(g, int) and g == 0:
        return Job(START0 + at)
    return Job(START1 + at, g - 1)


START_LAST = START1 + (GROUPS - 2) * len(FULL) + len(iteration_jobs(False, True))


def last_job(kind, i):
    return Job(START_LAST + LAST.index((FIN, kind, i)))


def o_place(j, parity):
    return j if j >= 2 else j + PAIRS * parity


def raw_place(t, parity):
    return t if t < 12 else t + 4 * parity


def build(nc, x, wq, wkv, wo, w1, w2, vectors, sel32, sel16, out):
    f32, f16, bf16, i32 = mybir.dt.float32, mybir.dt.float16, mybir.dt.bfloat16, mybir.dt.int32
    ALU = mybir.AluOpType
    ACT = mybir.ActivationFunctionType
    AX = mybir.AxisListType

    x_g = x.rearrange("(g s) (t p) d -> g p s t d", s=2, p=P)
    out_g = out.rearrange("(g s) (t p) d -> g p s t d", s=2, p=P)

    with ExitStack() as ctx:
        def sb(name, shape, dt=f32):
            return ctx.enter_context(nc.sbuf_tensor(name, shape, dt))

        def sem(name):
            return ctx.enter_context(nc.semaphore(name))

        consts = sb("consts", [P, P + 4 * 32 + PAIRS * 32 + 2])
        ident = consts[:, 0:P]
        sum_sel = consts[:, P:P + 128].rearrange("p (i m) -> p i m", i=4)
        den_sel = consts[:, 2 * P:2 * P + PAIRS * 32].rearrange("p (j m) -> p j m", j=PAIRS)
        neg_mask = consts[:, 2 * P + PAIRS * 32:2 * P + PAIRS * 32 + 2]
        spread = sb("spread", [P, 2, QKT, P], bf16)
        w_hi = sb("w_hi", [P, 3 * INNER], f16)
        w_lo = sb("w_lo", [P, 3 * INNER], f16)
        wo_sb = sb("wo_sb", [P, PAIRS, DIM])
        sgn1T = sb("sgn1T", [P, HIDDEN], f16)
        sgn2T = sb("sgn2T", [P, HT, P])
        small = sb("small", [P, VECS + HT + 1])
        gq, gk = small[:, 0:PAIRS], small[:, PAIRS:2 * PAIRS]
        b1_sb = small[:, 2 * PAIRS:2 * PAIRS + HT]
        b2_sb, nw = small[:, VECS - 2:VECS - 1], small[:, VECS - 1:VECS]
        alpha1, alpha2 = small[:, VECS:VECS + HT], small[:, VECS + HT:VECS + HT + 1]
        minus_half = sb("minus_half", [P, NTT])
        quarter = sb("quarter", [P, 2, NTT])
        x_in = sb("x_in", [P, NTT, DIM])
        stat1 = sb("stat1", [P, NTT, 6])
        mom1 = sb("mom1", [P, MOM, NTT])
        rms1 = sb("rms1", [P, NTT])
        xn = sb("xn", [P, NTT, DIM])
        xT_hi = sb("xT_hi", [P, TOK], f16)
        xT_lo = sb("xT_lo", [P, TOK], f16)
        raw = sb("raw", [P, QKT + 4, TOK])
        squares = sb("squares", [P, 4, TOK])
        sumsq = sb("sumsq", [P, TOK])
        rnorm = sb("rnorm", [P, TOK])
        newton = sb("newton", [P, TOK])
        part_n = sb("part_n", [P, TOK], bf16)
        rn3 = [sb(f"rn3_{b}", [P, TOK], bf16) for b in range(2)]
        v_sb = [sb(f"v_sb{b}", [P, NTT, INNER]) for b in range(2)]
        k_unit = [sb(f"k_unit{b}", [P, TOK]) for b in range(2)]
        q_unit = [sb(f"q_unit{b}", [P, TOK]) for b in range(2)]
        k_both = [sb(f"k_both{b}", [P, 2, TOK], f16) for b in range(2)]
        q_high = [sb(f"q_high{b}", [P, 2, TOK], f16) for b in range(2)]
        q_low = [sb(f"q_low{b}", [P, 2, TOK], f16) for b in range(2)]
        probs = [[sb(f"probs{b}{e}", [P, 2 * KT * SEQ]) for e in range(2)] for b in range(2)]
        key_sums = sb("key_sums", [P, 2, 2, SEQ])
        o_sb = sb("o_sb", [P, PAIRS + 2, TOK])
        rden = newton[:, 0:SEQ]
        part_d = part_n[:, 0:SEQ]
        rd3 = sb("rd3", [P, SEQ], bf16)
        residual = sb("residual", [P, NTT, DIM])
        turning = sb("turning", [P, TOK])
        x1 = sb("x1", [P, NTT, DIM])
        stat2 = sb("stat2", [P, NTT, 6])
        mom2 = sb("mom2", [P, MOM, NTT])
        rstd2 = sb("rstd2", [P, NTT])
        x2T_hi = sb("x2T_hi", [P, TOK], f16)
        x2T_lo = sb("x2T_lo", [P, TOK], f16)
        hid = sb("hid", [P, HT, TOK])
        out_sb = sb("out_sb", [P, NTT, DIM])

        score = ctx.enter_context(nc.psum_tensor("score", [P, 2, 2 * KT * SEQ], f32))
        work = ctx.enter_context(nc.psum_tensor("work", [P, 2, TOK], f32))
        o_ps = ctx.enter_context(nc.psum_tensor("o_ps", [P, TOK], f32))
        den_ps = ctx.enter_context(nc.psum_tensor("den_ps", [P, 2 * SEQ], f32))

        consts_loaded = sem("consts_loaded")
        vectors_loaded = sem("vectors_loaded")
        w_loaded = [sem("wq_loaded"), sem("wk_loaded"), sem("wv_loaded")]
        ffn_loaded = sem("ffn_loaded")
        spread_loaded = sem("spread_loaded")
        wo_loaded = sem("wo_loaded")
        scales_ready = sem("scales_ready")
        w_high = sem("w_high")
        w_low = sem("w_low")
        sign_steps = sem("sign_steps")
        signs_turned = sem("signs_turned")
        signs_taken = sem("signs_taken")
        zeros_ready = sem("zeros_ready")
        x_loaded = sem("x_loaded")
        res_loaded = sem("res_loaded")
        stored = sem("stored")
        work_full = sem("work_full")
        work_taken = [sem(f"work_taken{b}") for b in range(2)]
        row_stats1 = sem("row_stats1")
        moments1 = sem("moments1")
        rms1_ready = sem("rms1_ready")
        x_normed = sem("x_normed")
        rnorm_steps = sem("rnorm_steps")
        highs_ready = sem("highs_ready")
        k_lows_ready = sem("k_lows_ready")
        q_lows_ready = sem("q_lows_ready")
        rnorm_parts = sem("rnorm_parts")
        scores_full = sem("scores_full")
        scores_taken = sem("scores_taken")
        probs_ready = sem("probs_ready")
        sums_ready = sem("sums_ready")
        pv_done = sem("pv_done")
        o_taken = sem("o_taken")
        rden_parts = sem("rden_parts")
        row_stats2 = sem("row_stats2")
        moments2 = sem("moments2")
        rstd2_ready = sem("rstd2_ready")
        x1_normed = sem("x1_normed")
        gelu_done = sem("gelu_done")
        powers_ready = sem("powers_ready")
        early_sums = sem("early_sums")
        x_high = sem("x_high")
        x1_high = sem("x1_high")

        block = ctx.enter_context(nc.Block())
        SIGN_STEPS = 8
        W_PART_AT = [("qk", 0), ("qk", 1), ("v", 0)]
        w_raw = [probs[0][0], probs[0][1], probs[1][0]]
        w1_raw, w2_raw = probs[1][1][:, 0:HIDDEN], probs[1][1][:, HIDDEN:2 * HIDDEN]

        def taken(eng, job):
            eng.wait_ge(work_taken[job.bank], job.turn + 1)

        def run(eng, first, iteration, last):
            first()
            iteration(0, 0, True, False)
            with eng.Fori(0, (GROUPS - 4) // 2) as k:
                iteration(k * 2 + 1, 1, True, True)
                iteration(k * 2 + 2, 0, True, True)
            iteration(GROUPS - 3, 1, True, True)
            iteration(GROUPS - 2, 0, True, True)
            iteration(GROUPS - 1, 1, False, True)
            last()

        def vector_has_q_lows(group, j):
            return isinstance(group, int) and (group == 0 or (group == GROUPS - 1 and j >= 2))

        def group_follows(g, distance):
            return not isinstance(g, int) or g + distance < GROUPS

        @block.sync
        def _(sp):
            def load_x(g):
                sp.dma_start(x_in[:, :, :].rearrange("p (s t) d -> p s t d", s=2), x_g[g]).then_inc(x_loaded, 16)

            load_x(0)
            sp.dma_start(consts[:, :], sel32).then_inc(consts_loaded, 16)
            sp.dma_start(w_raw[1][:, :], wkv[:, 0:INNER]).then_inc(w_loaded[1], 16)
            sp.dma_start(w_raw[2][:, :], wkv[:, INNER:2 * INNER]).then_inc(w_loaded[2], 16)
            sp.dma_start(w2_raw, w2).then_inc(ffn_loaded, 16)

            def load_residual(g):
                sp.dma_start(residual[:, :, :].rearrange("p (s t) d -> p s t d", s=2), x_g[g]).then_inc(res_loaded, 16)

            def first():
                sp.dma_start(wo_sb[:, :, :], wo.rearrange("(j p) d -> p j d", p=P)).then_inc(wo_loaded, 16)
                sp.wait_ge(x_normed, NTT)
                load_x(1)

            def store(g):
                sp.dma_start(out_g[g], out_sb[:, :, :].rearrange("p (s t) d -> p s t d", s=2)).then_inc(stored, 16)

            def iteration(g, b, prep, fin):
                if group_follows(g, 2):
                    sp.wait_ge(x_normed, g * NTT + 2 * NTT)
                    load_x(g + 2)
                if fin:
                    taken(sp, job_of(g, "ty", 0, prep, fin))
                    store(g - 1)
                    sp.wait_ge(stored, g * 16)
                load_residual(g)

            def last():
                taken(sp, last_job("ty", 0))
                store(GROUPS - 1)
                sp.wait_ge(stored, 16 * GROUPS)

            run(sp, first, iteration, last)

        @block.gpsimd
        def _(pool):
            pool.memset(minus_half[:, :], -0.5).then_inc(powers_ready, 1)
            pool.memset(quarter[:, 0, :], 0.25 * (1.0 + RMS_EPS)).then_inc(powers_ready, 1)
            pool.memset(quarter[:, 1, :], 0.25).then_inc(powers_ready, 1)
            pool.wait_ge(powers_ready, 3)
            for b in range(2):
                pool.memset(q_low[b][DH:P, 0, :], 0.0).then_inc(zeros_ready, 1)
                pool.wait_ge(zeros_ready, 2 * b + 1)
                pool.memset(q_low[b][0:DH, 1, :], 0.0).then_inc(zeros_ready, 1)
                pool.wait_ge(zeros_ready, 2 * b + 2)

            def row_power(n, stat, mom, scaled, eps, row_stats, steps, ready, result):
                mean, diff, dev, var = (mom[:, i, :] for i in range(MOM))
                fourth = quarter[:, 0 if scaled != 1.0 else 1, :]
                tt, ts = nc.gpsimd.tensor_tensor, nc.gpsimd.tensor_scalar
                pool.wait_ge(row_stats, n * NTT + NTT)
                tt(mean, stat[:, :, 1], stat[:, :, 4], ALU.add).then_inc(steps, 1)
                tt(diff, stat[:, :, 1], stat[:, :, 4], ALU.subtract).then_inc(steps, 1)
                tt(dev, stat[:, :, 2], stat[:, :, 5], ALU.add).then_inc(steps, 1)
                pool.wait_ge(steps, n * STEPS + 3)
                tt(diff, diff, diff, ALU.mult).then_inc(steps, 1)
                ts(mean, mean, 0.5, None, ALU.mult).then_inc(steps, 1)
                ts(dev, dev, scaled / DIM, eps, ALU.mult, ALU.add).then_inc(steps, 1)
                pool.wait_ge(steps, n * STEPS + 6)
                tt(diff, diff, fourth, ALU.mult).then_inc(steps, 1)
                pool.wait_ge(steps, n * STEPS + 7)
                tt(var, dev, diff, ALU.add).then_inc(steps, 1)
                pool.wait_ge(steps, n * STEPS + 8)
                tt(result, var, minus_half[:, 0:NTT], ALU.pow).then_inc(ready, 1)
                pool.wait_ge(ready, n + 1)

            def ln1_power(n):
                row_power(n, stat1, mom1, 1.0 + RMS_EPS, RMS_EPS * LN_EPS, row_stats1, moments1, rms1_ready, rms1[:, :])

            def k_lows(g, j):
                pool.wait_ge(highs_ready, (g * PAIRS + j) * 6 + 2)
                for e in range(2):
                    own, far = slice(e * DH, (e + 1) * DH), slice((1 - e) * DH, (2 - e) * DH)
                    nc.gpsimd.tensor_tensor(k_both[j % 2][far, e, :], k_unit[j % 2][own, :], k_both[j % 2][own, e, :],
                                            ALU.subtract).then_inc(k_lows_ready, 1)
                pool.wait_ge(k_lows_ready, (g * PAIRS + j) * 2 + 2)

            def q_lows(g, j):
                pool.wait_ge(highs_ready, (g * PAIRS + j) * 6 + 4)
                for e in range(2):
                    own = slice(e * DH, (e + 1) * DH)
                    nc.gpsimd.tensor_tensor(q_low[j % 2][own, e, :], q_unit[j % 2][own, :], q_high[j % 2][own, e, :],
                                            ALU.subtract).then_inc(q_lows_ready, 1)
                pool.wait_ge(q_lows_ready, (g * PAIRS + j) * 2 + 2)

            def sums(g, j):
                for e in range(2):
                    pool.wait_ge(probs_ready, g * (2 * PAIRS) + (2 * j + e + 1))
                    if e == 0 and not (isinstance(g, int) and g == 0 and j == 0):
                        pool.wait_ge(pv_done, g * PAIRS + j)
                    tiles = probs[j % 2][e][:, :].rearrange("p (s k q) -> p s k q", s=2, k=KT)
                    nc.gpsimd.tensor_tensor(key_sums[:, e, :, :], tiles[:, :, 0, :], tiles[:, :, 1, :], ALU.add)\
                        .then_inc(sums_ready, 1)
                pool.wait_ge(sums_ready, g * (2 * PAIRS) + (2 * j + 2))

            def ln2_power(n):
                row_power(n, stat2, mom2, 1.0, LN_EPS, row_stats2, moments2, rstd2_ready, rstd2[:, :])

            def first():
                ln1_power(0)
                ln1_power(1)
                k_lows(0, 0)

            def iteration(g, b, prep, fin):
                for j in range(PAIRS):
                    for behind in ("lows", "sums"):
                        if behind == "sums":
                            sums(g, j)
                        elif j < PAIRS - 1 or prep:
                            pair = (g, j + 1) if j < PAIRS - 1 else (g + 1, 0)
                            k_lows(*pair)
                            if not vector_has_q_lows(*pair):
                                q_lows(*pair)
                        if group_follows(g, 2) and LN1_POWER_AT == (j, behind):
                            ln1_power(g + 2)
                        if fin and LN2_POWER_AT == (j, behind):
                            ln2_power(g - 1)

            def last():
                ln2_power(GROUPS - 1)

            run(pool, first, iteration, last)

        @block.scalar
        def _(act):
            act.dma_start(small[:, 0:VECS], vectors).then_inc(vectors_loaded, 16)
            act.dma_start(w_raw[0][:, :], wq).then_inc(w_loaded[0], 16)
            act.dma_start(w1_raw.rearrange("p (t d) -> p t d", t=HT), w1.rearrange("(t p) d -> p t d", p=P))\
                .then_inc(ffn_loaded, 16)
            act.dma_start(spread[:, :, :, :].rearrange("p a t m -> p (a t m)"), sel16).then_inc(spread_loaded, 16)
            act.wait_ge(scales_ready, 1)
            for part in range(3):
                act.wait_ge(w_loaded[part], 16)
                nc.scalar.activation(w_hi[:, part * INNER:(part + 1) * INNER], w_raw[part][:, :], ACT.Copy, scale=nw)\
                    .then_inc(w_high, 1)

            def take(job, kind, i, parity):
                bank = work[:, job.bank, :]
                act.wait_ge(work_full, job.number + 1)
                if kind == "v":
                    t, c = i // 2, (i % 2) * TOK
                    last_read = nc.scalar.activation(v_sb[parity][:, t, c:c + TOK], bank, ACT.Copy, scale=1.0 / WSCALE)
                else:
                    nc.scalar.activation(raw[:, raw_place(i, parity), :], bank, ACT.Copy)
                    last_read = nc.scalar.activation(squares[:, i % 4, :], bank, ACT.Square)
                last_read.then_inc(work_taken[job.bank], 1)

            def gelu(n, last_h):
                taken(act, last_h)
                nc.scalar.activation(hid[:, :, :], hid[:, :, :], ACT.Gelu).then_inc(gelu_done, 1)

            def take_o(g, j, parity):
                act.wait_ge(pv_done, g * PAIRS + (j + 1))
                nc.scalar.activation(o_sb[:, o_place(j, parity), :], o_ps[:, :], ACT.Copy).then_inc(o_taken, 1)

            def first():
                for n, (_, kind, i) in enumerate(FIRST):
                    if kind in BY_SCALAR:
                        take(Job(n), kind, i, 0)

            def iteration(g, b, prep, fin):
                def takes(slot, phase):
                    for _, kind, i in slot_jobs(slot, prep, fin)[phase]:
                        if kind in BY_SCALAR:
                            take(job_of(g, kind, i, prep, fin), kind, i, 1 - b)
                    if fin and (slot, phase) == GELU_AT:
                        gelu(g - 1, job_of(g, "h", HT - 1, prep, fin))

                for j in range(PAIRS):
                    takes(j, 0)
                    for e in range(2):
                        takes(j, 1 + 2 * e)
                        act.wait_ge(scores_full, g * (2 * PAIRS) + (2 * j + e + 1))
                        if not (isinstance(g, int) and g == 0 and j < 2):
                            act.wait_ge(pv_done, g * PAIRS + (j - 1))
                        nc.scalar.activation(probs[j % 2][e][:, :], score[:, e, :], ACT.Tanh,
                                             scale=1.0 / SOFTCLAMP).then_inc(scores_taken, 1)
                        takes(j, 2 + 2 * e)
                    for e in range(2):
                        act.wait_ge(scores_taken, g * (2 * PAIRS) + (2 * j + e + 1))
                        nc.scalar.activation(probs[j % 2][e][:, :], probs[j % 2][e][:, :], ACT.Exp,
                                             scale=SOFTCLAMP * DH ** -0.5).then_inc(probs_ready, 1)
                        takes(j, 5 + e)
                    if j:
                        take_o(g, j - 1, b)
                    elif not (isinstance(g, int) and g == 0):
                        take_o(g - 1, PAIRS - 1, 1 - b)

            def last():
                take_o(GROUPS - 1, PAIRS - 1, 1)
                gelu(GROUPS - 1, last_job("h", HT - 1))

            run(act, first, iteration, last)

        @block.tensor
        def _(pe):
            def turn_signs():
                pe.wait_ge(sign_steps, SIGN_STEPS)
                for n, signs in enumerate((w1_raw, w2_raw)):
                    for t in range(HT):
                        cols = slice(t * P, (t + 1) * P)
                        last_turn = nc.tensor.transpose(score[:, n, cols], signs[:, cols], ident)
                last_turn.then_inc(signs_turned, 1)

            def wo_step(j, parity, bank):
                return nc.tensor.matmul(bank, wo_sb[:, j, :], o_sb[:, o_place(j, parity), :], start=(j == 0),
                                        stop=(j == PAIRS - 1))

            def job(this, find, kind, i, group, parity):
                bank = work[:, this.bank, :]
                if not (isinstance(this.turn, int) and this.turn == 0):
                    pe.wait_ge(work_taken[this.bank], this.turn)

                def needs(*earlier):
                    others = [of for of in earlier if of.bank != this.bank]
                    if others:
                        taken(pe, max(others, key=lambda of: of.at))

                if kind == "x":
                    if isinstance(group, int) and group == 0:
                        pe.wait_ge(consts_loaded, 16)
                    pe.wait_ge(x_normed, group * NTT + NTT)
                    for t in range(NTT):
                        mm = nc.tensor.transpose(bank[:, t * P:(t + 1) * P], xn[:, t, :], ident)
                elif kind == "qk":
                    needs(find("x", 0))
                    col = (i % 2) * INNER + (i // 2) * P
                    for s, (w, xt) in enumerate(((w_hi, xT_hi), (w_hi, xT_lo), (w_lo, xT_hi))):
                        mm = nc.tensor.matmul(bank, w[:, col:col + P], xt[:, :], start=(s == 0), stop=(s == 2))
                elif kind == "v":
                    needs(find("x", 0))
                    t, c = i // 2, 2 * INNER + (i % 2) * TOK
                    for s, (xt, w) in enumerate(((xT_hi, w_hi), (xT_lo, w_hi), (xT_hi, w_lo))):
                        mm = nc.tensor.matmul(bank, xt[:, t * P:(t + 1) * P], w[:, c:c + TOK],
                                              start=(s == 0), stop=(s == 2))
                elif kind == "ss":
                    needs(*(find("qk", t) for t in range(4 * i, 4 * i + 4)))
                    for c in range(4):
                        mm = nc.tensor.matmul(bank[32 * c:32 * c + 32, :], sum_sel[:, i, :], squares[:, c, :],
                                              start=True, stop=True)
                elif kind in ("nq", "nk"):
                    pe.wait_ge(rnorm_parts, 5 if early(group, i) else group * 5 + 10)
                    parts = rn3[1] if early(group, i) else rn3[parity]
                    mm = nc.tensor.matmul(bank, spread[:, 0, 2 * i + (kind == "nk"), :], parts[:, :], start=True,
                                          stop=True)
                elif kind == "ob":
                    pe.wait_ge(rden_parts, group * 6 + 6)
                    for s in range(2):
                        mm = nc.tensor.matmul(bank[:, s * SEQ:(s + 1) * SEQ], spread[:, 1, 2 * i + s, :], rd3[:, :],
                                              start=True, stop=True)
                elif kind == "wo":
                    needs(*(find("ob", j) for j in range(PAIRS)))
                    for j in range(PAIRS):
                        mm = wo_step(j, parity, bank)
                elif kind == "ta":
                    needs(find("wo", 0))
                    for t in range(NTT):
                        mm = nc.tensor.transpose(bank[:, t * P:(t + 1) * P], turning[:, t * P:(t + 1) * P], ident)
                elif kind == "t2":
                    pe.wait_ge(x1_normed, group * NTT + NTT)
                    for t in range(NTT):
                        mm = nc.tensor.transpose(bank[:, t * P:(t + 1) * P], residual[:, t, :], ident)
                elif kind == "h":
                    needs(find("t2", 0))
                    for s, xt in enumerate((x2T_hi, x2T_lo)):
                        mm = nc.tensor.matmul(bank, sgn1T[:, i * P:(i + 1) * P], xt[:, :], start=(s == 0),
                                              stop=(s == 1))
                elif kind == "y":
                    pe.wait_ge(gelu_done, group + 1)
                    for t in range(HT):
                        mm = nc.tensor.matmul(bank, sgn2T[:, t, :], hid[:, t, :], start=(t == 0), stop=(t == HT - 1))
                elif kind == "ty":
                    needs(find("y", 0))
                    for t in range(NTT):
                        mm = nc.tensor.transpose(bank[:, t * P:(t + 1) * P], turning[:, t * P:(t + 1) * P], ident)
                mm.then_inc(work_full, 1)

            def scores(g, j, e, s):
                if e == 0 and s == 0:
                    pe.wait_ge(highs_ready, (g * PAIRS + j) * 6 + 6)
                    pe.wait_ge(k_lows_ready, (g * PAIRS + j) * 2 + 2)
                    pe.wait_ge(q_lows_ready, (g * PAIRS + j) * 2 + 2)
                if s == 0 and not (isinstance(g, int) and g == 0 and j == 0):
                    pe.wait_ge(scores_taken, g * (2 * PAIRS) + (2 * j + e - 1))
                for kt in range(KT):
                    c = (s * KT + kt) * SEQ
                    keys = k_both[j % 2][:, e, s * SEQ + kt * P:s * SEQ + (kt + 1) * P]
                    nc.tensor.matmul(score[:, e, c:c + SEQ], keys, q_high[j % 2][:, e, s * SEQ:(s + 1) * SEQ],
                                     start=True, stop=False)
                    mm = nc.tensor.matmul(score[:, e, c:c + SEQ], keys,
                                          q_low[j % 2][:, e, s * SEQ:(s + 1) * SEQ], start=False, stop=True)
                if s == 1:
                    mm.then_inc(scores_full, 1)

            def values(g, j, parity, s):
                if s == 0:
                    pe.wait_ge(probs_ready, g * (2 * PAIRS) + (2 * j + 2))
                    if not (isinstance(g, int) and g == 0 and j == 0):
                        pe.wait_ge(o_taken, g * PAIRS + j)
                for kt in range(KT):
                    c = (s * KT + kt) * SEQ
                    for e in range(2):
                        nc.tensor.matmul(o_ps[e * DH:(e + 1) * DH, s * SEQ:(s + 1) * SEQ],
                                         v_sb[parity][:, s * KT + kt, (2 * j + e) * DH:(2 * j + e + 1) * DH],
                                         probs[j % 2][e][:, c:c + SEQ], start=(kt == 0), stop=(kt == KT - 1))

            def denominators(g, j):
                if j == 0 and not (isinstance(g, int) and g == 0):
                    pe.wait_ge(rden_parts, g * 6 - 5)
                pe.wait_ge(sums_ready, g * (2 * PAIRS) + (2 * j + 2))
                for s in range(2):
                    for e in range(2):
                        q = 32 * (2 * e + s)
                        mm = nc.tensor.matmul(den_ps[q:q + 32, 0:SEQ], den_sel[:, j, :], key_sums[:, e, s, :],
                                              start=(j == 0), stop=(j == PAIRS - 1))
                mm.then_inc(pv_done, 1)

            def first():
                for n, (_, kind, i) in enumerate(FIRST):
                    if (kind, i) in W_PART_AT:
                        pe.wait_ge(w_low, 1 + W_PART_AT.index((kind, i)))
                    if (kind, i) == ("nq", 0):
                        pe.wait_ge(spread_loaded, 16)
                    if (kind, i) == ("v", 3):
                        turn_signs()
                    job(Job(n), first_job, kind, i, 0, 0)
                pe.wait_ge(wo_loaded, 16)
                pe.wait_ge(signs_taken, 2)

            def iteration(g, b, prep, fin):
                def find(kind, i):
                    return job_of(g, kind, i, prep, fin)

                def jobs(part):
                    for kind_of, kind, i in part:
                        group = {NORM: g, PREP: g + 1, FIN: g - 1}[kind_of]
                        job(find(kind, i), find, kind, i, group, b if kind_of == NORM else 1 - b)

                for j in range(PAIRS):
                    phases = slot_jobs(j, prep, fin)
                    unit = (g, j - 1, b) if j else (g - 1, PAIRS - 1, 1 - b)
                    has_unit = j > 0 or not (isinstance(g, int) and g == 0)
                    jobs(phases[0])
                    for e in range(2):
                        for s in range(2):
                            scores(g, j, e, s)
                            jobs(phases[1 + 2 * e + s])
                    for s in range(2):
                        if has_unit:
                            values(*unit, s)
                        jobs(phases[5 + s])
                    if has_unit:
                        denominators(unit[0], unit[1])

            def last():
                for s in range(2):
                    values(GROUPS - 1, PAIRS - 1, 1, s)
                denominators(GROUPS - 1, PAIRS - 1)
                for _, kind, i in LAST:
                    if kind == "wo":
                        taken(pe, last_job("ob", PAIRS - 1))
                        wo_step(PAIRS - 1, 1, o_ps[:, :]).then_inc(work_full, 1)
                        continue
                    job(last_job(kind, i), last_job, kind, i, GROUPS - 1, 1)
                    if kind == "ob" and i == 1:
                        pe.wait_ge(o_taken, GROUPS * PAIRS)
                    if kind == "ob" and i:
                        taken(pe, last_job("ob", i - 1))
                        wo_step(i - 1, 1, o_ps[:, :])

            run(pe, first, iteration, last)

        @block.vector
        def _(dve):
            def scales():
                dve.wait_ge(vectors_loaded, 16)
                nc.vector.tensor_scalar(nw, nw, WSCALE, None, ALU.mult).then_inc(scales_ready, 1)
                nc.vector.tensor_scalar(gq, gq, 1.0, DH ** 0.5, ALU.add, ALU.mult).then_inc(scales_ready, 1)
                nc.vector.tensor_scalar(gk, gk, 1.0, DH ** 0.5, ALU.add, ALU.mult).then_inc(scales_ready, 1)
                dve.wait_ge(scales_ready, 3)

            def weights_low(part):
                dve.wait_ge(w_high, part + 1)
                cols = slice(part * INNER, (part + 1) * INNER)
                nc.vector.scalar_tensor_tensor(w_lo[:, cols], w_raw[part][:, :], nw, w_hi[:, cols], ALU.mult,
                                               ALU.subtract).then_inc(w_low, 1)

            def signs():
                dve.wait_ge(ffn_loaded, 32)
                neg1, neg2 = hid[:, 0, :], hid[:, 1, :]
                nc.vector.tensor_reduce(alpha1, w1_raw.rearrange("p (t d) -> p t d", t=HT), AX.X, ALU.add,
                                        apply_absolute_value=True).then_inc(sign_steps, 1)
                nc.vector.tensor_reduce(alpha2, w2_raw, AX.X, ALU.add, apply_absolute_value=True)\
                    .then_inc(sign_steps, 1)
                nc.vector.tensor_scalar(neg1, w1_raw, 0.0, None, ALU.is_lt).then_inc(sign_steps, 1)
                nc.vector.tensor_scalar(neg2, w2_raw, 0.0, None, ALU.is_lt).then_inc(sign_steps, 1)
                dve.wait_ge(sign_steps, 4)
                nc.vector.tensor_scalar(alpha1, alpha1, 1.0 / DIM, None, ALU.mult).then_inc(sign_steps, 1)
                nc.vector.tensor_scalar(alpha2, alpha2, 1.0 / HIDDEN, None, ALU.mult).then_inc(sign_steps, 1)
                nc.vector.scalar_tensor_tensor(w1_raw, w1_raw, 0.0, neg1, ALU.is_gt, ALU.subtract)\
                    .then_inc(sign_steps, 1)
                nc.vector.scalar_tensor_tensor(w2_raw, w2_raw, 0.0, neg2, ALU.is_gt, ALU.subtract)\
                    .then_inc(sign_steps, 1)

            def signs_out():
                dve.wait_ge(signs_turned, 1)
                nc.vector.tensor_copy(sgn1T[:, :], score[:, 0, 0:HIDDEN]).then_inc(signs_taken, 1)
                nc.vector.tensor_copy(sgn2T[:, :, :].rearrange("p t m -> p (t m)"), score[:, 1, 0:HT * P])\
                    .then_inc(signs_taken, 1)

            def ln1_stats(n):
                dve.wait_ge(x_loaded, n * 16 + 16)
                for t in range(NTT):
                    nc.vector.bn_stats(stat1[:, t, :], x_in[:, t, :]).then_inc(row_stats1, 1)

            def ln1_apply(n):
                dve.wait_ge(rms1_ready, n + 1)
                for t in range(NTT):
                    nc.vector.tensor_scalar(xn[:, t, :], x_in[:, t, :], mom1[:, 0, t:t + 1], rms1[:, t:t + 1],
                                            ALU.subtract, ALU.mult).then_inc(x_normed, 1)

            def split3(target, part, rows, counter, base, steps):
                for step in steps:
                    if not (isinstance(base, int) and base + step == 0):
                        dve.wait_ge(counter, base + step)
                    if step in (0, 2):
                        nc.vector.tensor_copy(part, rows).then_inc(counter, 1)
                    elif step in (1, 3):
                        nc.vector.scalar_tensor_tensor(rows, part, neg_mask[:, step // 2:step // 2 + 1], rows, ALU.mult,
                                                       ALU.add).then_inc(counter, 1)
                    else:
                        nc.vector.tensor_copy(target, rows).then_inc(counter, 1)

            def norm_guess(last_ss):
                taken(dve, last_ss)
                nc.vector.tensor_scalar(rnorm[:, :].bitcast(i32), sumsq[:, :].bitcast(i32), -0.5, float(RSQRT_MAGIC),
                                        ALU.mult, ALU.add).then_inc(rnorm_steps, 1)

            def norm_newton(norm_round, step):
                dve.wait_ge(rnorm_steps, norm_round * NEWTON_STEPS + (step + 1))
                if step % 3 == 0:
                    nc.vector.scalar_tensor_tensor(newton[:, :], rnorm[:, :], -0.5, rnorm[:, :], ALU.mult, ALU.mult)\
                        .then_inc(rnorm_steps, 1)
                elif step % 3 == 1:
                    sums = turning if isinstance(norm_round, int) and norm_round == 0 else sumsq
                    nc.vector.tensor_tensor(newton[:, :], newton[:, :], sums[:, :], ALU.mult).then_inc(rnorm_steps, 1)
                else:
                    nc.vector.scalar_tensor_tensor(rnorm[:, :], newton[:, :], 1.5, rnorm[:, :], ALU.add, ALU.mult)\
                        .then_inc(rnorm_steps, 1)

            def norm_parts(norm_round, parity, steps):
                if 0 in steps:
                    dve.wait_ge(rnorm_steps, norm_round * NEWTON_STEPS + NEWTON_STEPS)
                split3(rn3[parity][:, :], part_n[:, :], rnorm[:, :], rnorm_parts, norm_round * 5, steps)

            def halves(g, j):
                b = j % 2
                u = g * PAIRS + j
                for unit, high in ((k_unit, k_both), (q_unit, q_high)):
                    for e in range(2):
                        own = slice(e * DH, (e + 1) * DH)
                        nc.vector.tensor_copy(high[b][own, e, :], unit[b][own, :]).then_inc(highs_ready, 1)
                dve.wait_ge(highs_ready, u * 6 + 4)
                with_lows = vector_has_q_lows(g, j)
                if with_lows and g == GROUPS - 1 and j == 2:
                    dve.wait_ge(k_lows_ready, u * 2 + 1)
                if with_lows:
                    for e in range(2):
                        own = slice(e * DH, (e + 1) * DH)
                        nc.vector.tensor_tensor(q_low[b][own, e, :], q_unit[j % 2][own, :], q_high[b][own, e, :],
                                                ALU.subtract).then_inc(q_lows_ready, 1)
                for e in range(2):
                    own, far = slice(e * DH, (e + 1) * DH), slice((1 - e) * DH, (2 - e) * DH)
                    nc.vector.tensor_copy(q_high[b][far, e, :], q_high[b][own, e, :]).then_inc(highs_ready, 1)

            def den_reciprocal(n):
                dve.wait_ge(pv_done, n * PAIRS + PAIRS)
                nc.vector.reciprocal(rden, den_ps[:, 0:SEQ]).then_inc(rden_parts, 1)

            def den_parts(n, steps):
                split3(rd3[:, :], part_d, rden, rden_parts, n * 6 + 1, steps)

            def take(job, kind, i, group, parity):
                alone = kind == "wo" and isinstance(group, int) and group == GROUPS - 1
                bank = o_ps[:, :] if alone else work[:, job.bank, :]
                dve.wait_ge(work_full, job.number + 1)
                if kind in ("x", "t2"):
                    hi, lo = (xT_hi, xT_lo) if kind == "x" else (x2T_hi, x2T_lo)
                    high_ready = x_high if kind == "x" else x1_high
                    nc.vector.tensor_copy(hi[:, :], bank).then_inc(high_ready, 1)
                    dve.wait_ge(high_ready, group + 1)
                    last = nc.vector.tensor_tensor(lo[:, :], bank, hi[:, :], ALU.subtract)
                elif kind == "ss":
                    floor = (NORM_FLOOR * WSCALE) ** 2
                    if i == 0:
                        last = nc.vector.tensor_scalar(sumsq[:, :], bank, floor, None, ALU.max)
                    else:
                        last = nc.vector.scalar_tensor_tensor(sumsq[:, :], bank, floor, sumsq[:, :], ALU.max, ALU.max)
                elif kind in ("nq", "nk"):
                    unit, gamma, t = (q_unit, gq, 2 * i) if kind == "nq" else (k_unit, gk, 2 * i + 1)
                    if kind == "nq" and not (isinstance(group, int) and group == 0 and i < 2):
                        dve.wait_ge(k_lows_ready, (group * PAIRS + i - 1) * 2)
                        dve.wait_ge(q_lows_ready, (group * PAIRS + i - 1) * 2)
                    last = nc.vector.scalar_tensor_tensor(unit[i % 2][:, :], bank, gamma[:, i:i + 1],
                                                          raw[:, raw_place(t, parity), :], ALU.mult, ALU.mult)
                elif kind == "ob":
                    dve.wait_ge(o_taken, group * PAIRS + (i + 1))
                    o = o_sb[:, o_place(i, parity), :]
                    last = nc.vector.tensor_tensor(o, o, bank, ALU.mult)
                elif kind == "wo":
                    last = nc.vector.tensor_copy(turning[:, :], bank)
                elif kind == "ta":
                    dve.wait_ge(res_loaded, group * 16 + 16)
                    last = nc.vector.tensor_tensor(x1[:, :, :].rearrange("p t d -> p (t d)"), bank,
                                                   residual[:, :, :].rearrange("p t d -> p (t d)"), ALU.add)
                elif kind == "h":
                    last = nc.vector.tensor_scalar(hid[:, i, :], bank, alpha1[:, i:i + 1], b1_sb[:, i:i + 1],
                                                   ALU.mult, ALU.add)
                elif kind == "y":
                    last = nc.vector.tensor_scalar(turning[:, :], bank, alpha2, b2_sb, ALU.mult, ALU.add)
                elif kind == "ty":
                    last = nc.vector.tensor_tensor(out_sb[:, :, :].rearrange("p t d -> p (t d)"), bank,
                                                   x1[:, :, :].rearrange("p t d -> p (t d)"), ALU.add)
                last.then_inc(work_taken[job.bank], 1)
                if kind == "ta":
                    ln2(job, group)
                if kind == "ss" and i == SS_ORDER[-1]:
                    norm_guess(job)

            def ln2(job, group):
                taken(dve, job)
                for t in range(NTT):
                    nc.vector.bn_stats(stat2[:, t, :], x1[:, t, :]).then_inc(row_stats2, 1)

            def ln2_apply(group):
                dve.wait_ge(rstd2_ready, group + 1)
                for t in range(NTT):
                    nc.vector.tensor_scalar(residual[:, t, :], x1[:, t, :], mom2[:, 0, t:t + 1], rstd2[:, t:t + 1],
                                            ALU.subtract, ALU.mult).then_inc(x1_normed, 1)

            def first():
                ln1_stats(0)
                scales()
                ln1_apply(0)
                weights_low(0)
                dve.wait_ge(consts_loaded, 16)
                for n, (_, kind, i) in enumerate(FIRST):
                    if kind not in BY_SCALAR:
                        take(Job(n), kind, i, 0, 0)
                    if kind == "x":
                        weights_low(1)
                        weights_low(2)
                        signs()
                    if (kind, i) == ("ss", 1):
                        norm_guess(Job(n))
                        nc.vector.tensor_copy(turning[:, :], sumsq[:, :]).then_inc(early_sums, 1)
                        dve.wait_ge(early_sums, 1)
                        for step in range(5):
                            norm_newton(0, step)
                    if (kind, i) == ("ss", 3):
                        for step in range(5, 9):
                            norm_newton(0, step)
                        norm_parts(0, 1, range(5))
                        ln1_stats(1)
                    if kind == "nk":
                        units_landed(first_job("nq", i), first_job("nk", i))
                        halves(0, i)
                signs_out()
                ln1_apply(1)

            def units_landed(*jobs):
                for job in jobs:
                    taken(dve, job)

            def iteration(g, b, prep, fin):
                def takes(part):
                    for kind_of, kind, i in part:
                        if kind in BY_SCALAR:
                            continue
                        if kind == "t2":
                            ln2_apply(g - 1)
                        group = {NORM: g, PREP: g + 1, FIN: g - 1}[kind_of]
                        take(job_of(g, kind, i, prep, fin), kind, i, group, b if kind_of == NORM else 1 - b)
                        if kind == "nk":
                            units_landed(job_of(g, "nq", i, prep, fin), job_of(g, "nk", i, prep, fin))
                            halves(group, i)

                for j in range(PAIRS):
                    phases = slot_jobs(j, prep, fin)
                    for phase in range(PHASES):
                        takes(phases[phase])
                        place = PHASES * j + phase
                        if isinstance(g, int) and g == 0 and 1 <= place <= 10:
                            if place < 10:
                                norm_newton(1, place - 1)
                            else:
                                norm_parts(1, 0, range(5))
                        for what in VECTOR_WORK.get((j, phase), ()):
                            step = int(what[-1]) if what[-1].isdigit() else 0
                            if what.startswith("den"):
                                if not (isinstance(g, int) and g == 0):
                                    if what == "den_reciprocal":
                                        den_reciprocal(g - 1)
                                    else:
                                        den_parts(g - 1, PART_STEPS[step])
                            elif what in ("stats", "apply"):
                                if group_follows(g, 2):
                                    (ln1_stats if what == "stats" else ln1_apply)(g + 2)
                            elif prep:
                                if what.startswith("parts"):
                                    norm_parts(g + 2, 1 - b, PART_STEPS[step])
                                else:
                                    norm_newton(g + 2, step)

            def last():
                den_reciprocal(GROUPS - 1)
                den_parts(GROUPS - 1, range(5))
                for _, kind, i in LAST:
                    if kind == "t2":
                        ln2_apply(GROUPS - 1)
                    take(last_job(kind, i), kind, i, GROUPS - 1, 1)

            run(dve, first, iteration, last)


def constants():
    import numpy as np
    s32 = np.zeros((P, P + 128 + PAIRS * 32 + 2), np.float32)
    s32[:, 0:P] = np.eye(P)
    for i in range(4):
        for k in range(4):
            for e in range(2):
                s32[e * DH:(e + 1) * DH, P + i * 32 + 8 * k + 2 * i + e] = 1.0
    for j in range(PAIRS):
        s32[:, 2 * P + 32 * j + j:2 * P + 32 * j + 32:8] = 1.0
    block = (np.arange(P) // 8) % 4
    s32[:, -2] = -1.0 * (block >= 1)
    s32[:, -1] = -1.0 * (block >= 2)
    s16 = np.zeros((P, 2, QKT, P), np.float32)
    for k in range(3):
        for e in range(2):
            cols = slice(e * DH, (e + 1) * DH)
            for t in range(QKT):
                s16[32 * (t % 4) + 8 * k + 2 * (t // 4) + e, 0, t, cols] = 1.0
            for j in range(PAIRS):
                for s in range(2):
                    s16[32 * (2 * e + s) + 8 * k + j, 1, 2 * j + s, cols] = 1.0
    return s32, s16.reshape(P, -1)


def vectors_by_partition(norm_w, q_gamma, k_gamma, b1, b2):
    import numpy as np
    return np.ascontiguousarray(np.concatenate([
        q_gamma.reshape(PAIRS, P).T, k_gamma.reshape(PAIRS, P).T, b1.reshape(HT, P).T,
        b2.reshape(P, 1), norm_w.reshape(P, 1)], axis=1))


def kernel(L0_attn_tokens, L0_attn_norm_w, L0_attn_Wq, L0_attn_Wkv, L0_attn_Wo, L0_attn_q_gamma, L0_attn_k_gamma,
           L0_ffn_w1, L0_ffn_b1, L0_ffn_w2, L0_ffn_b2):
    import numpy as _np
    import ml_dtypes as _ml
    import concourse.bacc as _bacc
    from concourse import mybir as _mybir
    from concourse.bass_utils import run_bass_kernel_spmd as _run

    nc = _bacc.Bacc("TRN2", target_bir_lowering=False, num_devices=1)
    s32, s16 = constants()
    small = [_np.asarray(a) for a in (L0_attn_norm_w, L0_attn_q_gamma, L0_attn_k_gamma, L0_ffn_b1, L0_ffn_b2)]
    given = {
        "tokens": L0_attn_tokens, "Wq": L0_attn_Wq, "Wkv": L0_attn_Wkv, "Wo": L0_attn_Wo,
        "w1": L0_ffn_w1, "w2": L0_ffn_w2, "vectors": vectors_by_partition(*small),
        "sel32": s32, "sel16": s16.astype(_ml.bfloat16),
    }
    arrays, args = {}, []
    for name, a in given.items():
        a = _np.ascontiguousarray(a)
        arrays[f"in_{name}_dram"] = a
        args.append(nc.dram_tensor(f"in_{name}_dram", a.shape, _mybir.dt.from_np(a.dtype), kind="ExternalInput").ap())
    out = nc.dram_tensor("out_dram", (BATCH, SEQ, DIM), _mybir.dt.float32, kind="ExternalOutput").ap()
    build(nc, *args, out)
    r = _run(nc, [arrays], core_ids=[0])
    return r.results[0]["out_dram"]
```
